# Optimizing a Trainium2 kernel written in Bass

```python
import numpy as np
import jax
import jax.numpy as jnp

def _softmax(x, axis=-1):
    return jax.nn.softmax(x, axis=axis)

def _gelu(x):
    return jax.nn.gelu(x, approximate=True)

def _silu(x):
    return jax.nn.silu(x)

def _sigmoid(x):
    return jax.nn.sigmoid(x)

def _layernorm(x, axis=-1, eps=1e-05):
    m = jnp.mean(x, axis=axis, keepdims=True)
    v = jnp.var(x, axis=axis, keepdims=True)
    return (x - m) / jnp.sqrt(v + eps)

def _scatter_add(tgt, idx, src, axis=0):
    return tgt.at[idx].add(src)

def _segment_sum(src, seg, n):
    return jax.ops.segment_sum(src, seg, n)
kernel_name = 'mk_decoder_preln_d2_seqx_r8_27bf03'

def setup_inputs(seed: int=0):
    np.random.seed(seed)
    _w = jnp.asarray

    def _rec_inputs():
        import jax
        import jax.numpy as jnp
        _rk = jax.random.key(seed)
        x = -0.0002928 + 1 * jax.random.normal(jax.random.fold_in(_rk, 1), (8, 256, 128), jnp.float32)
        _lenS = 256 - jax.random.randint(jax.random.fold_in(_rk, 7), (8,), 0, max(1, 256 // 4) + 1, jnp.int32)
        _lenS2 = 64 - jax.random.randint(jax.random.fold_in(_rk, 8), (8,), 0, max(1, 64 // 4) + 1, jnp.int32)
        _ctx_1024P = jax.random.normal(jax.random.fold_in(_rk, 11), (8, 16, 128), jnp.float32)
        _ctx_1024c = jax.random.dirichlet(jax.random.fold_in(_rk, 511), 0.3 * jnp.ones((16,), jnp.float32), (8, 64))
        _ctx_1024t = jnp.einsum('bsk,bkd->bsd', _ctx_1024c, _ctx_1024P)
        _ctx_1024t = _ctx_1024t * jax.lax.rsqrt(jnp.mean(jnp.square(_ctx_1024t)) + 1e-12) * 0.953939
        ctx_1024 = -1.39393e-06 + 0.999914 * (_ctx_1024t + 0.3 * jax.random.normal(jax.random.fold_in(_rk, 611), (8, 64, 128), jnp.float32))
        return (x, ctx_1024)
    x, ctx_1024 = _rec_inputs()

    def _L0_attn_setup():
        import jax, jax.numpy as jnp
        import numpy as np
        B, L, D, S = (4, 256, 128, 16)
        key = jax.random.key(seed)
        ks = jax.random.split(key, 8)
        inv_d = 1.0 / np.sqrt(D)
        inv_s = 1.0 / np.sqrt(S)
        A_log = jnp.broadcast_to(jnp.clip(jnp.log(jnp.arange(1, S + 1, dtype=jnp.float32)), -7.0, None), (D, S))
        return {'x': jax.random.normal(ks[0], (B, L, D), jnp.float32), 'A_log': A_log, 'W_B': jax.random.uniform(ks[1], (S, D), jnp.float32, -inv_d, inv_d), 'W_C': jax.random.uniform(ks[2], (D, S), jnp.float32, -inv_s, inv_s), 'D_skip': jnp.ones((D,), jnp.float32), 'log_dt': jax.random.normal(ks[3], (D,), jnp.float32) * 0.01 - 4.0, 'W_in': jax.random.uniform(ks[4], (2 * D, D), jnp.float32, -inv_d, inv_d), 'b_in': jax.random.uniform(ks[5], (2 * D,), jnp.float32, -inv_d, inv_d), 'W_out': jax.random.uniform(ks[6], (D, D), jnp.float32, -inv_d, inv_d), 'b_out': jax.random.uniform(ks[7], (D,), jnp.float32, -inv_d, inv_d), 'ln_g': jnp.ones((D,), jnp.float32), 'ln_b': jnp.zeros((D,), jnp.float32)}
    _L0_attn_all = _L0_attn_setup()
    _L0_attn_in = {k: v for k, v in _L0_attn_all.items() if k in ('A_log', 'W_B', 'W_C', 'D_skip', 'log_dt', 'W_in', 'b_in', 'W_out', 'b_out', 'ln_g', 'ln_b')}
    del _L0_attn_all

    def _L0_xattn_setup():
        import jax, jax.numpy as jnp
        import numpy as np
        D_MODEL = 128
        N_HEADS = 16
        D_K = D_MODEL // N_HEADS

        def _xavier(key, shape):
            fan_in, fan_out = (shape[1], shape[0])
            a = float(np.sqrt(6.0 / (fan_in + fan_out)))
            return jax.random.uniform(key, shape, jnp.float32, -a, a)
        key = jax.random.key(seed)
        ks = jax.random.split(key, 7)
        B, S = (2, 256)
        return {'query': jax.random.normal(ks[0], (B, S, D_MODEL), jnp.float32), 'key': jax.random.normal(ks[1], (B, S, D_MODEL), jnp.float32), 'value': jax.random.normal(ks[2], (B, S, D_MODEL), jnp.float32), 'w_q': _xavier(ks[3], (D_MODEL, D_MODEL)), 'w_k': _xavier(ks[4], (D_MODEL, D_MODEL)), 'w_v': _xavier(ks[5], (D_MODEL, D_MODEL)), 'w_o': _xavier(ks[6], (D_MODEL, D_MODEL)), 'b_q': jnp.zeros((D_MODEL,), jnp.float32), 'b_k': jnp.zeros((D_MODEL,), jnp.float32), 'b_v': jnp.zeros((D_MODEL,), jnp.float32), 'b_o': jnp.zeros((D_MODEL,), jnp.float32)}
    _L0_xattn_all = _L0_xattn_setup()
    _L0_xattn_in = {k: v for k, v in _L0_xattn_all.items() if k in ('w_q', 'w_k', 'w_v', 'w_o', 'b_q', 'b_k', 'b_v', 'b_o')}
    del _L0_xattn_all

    def _L0_ffn_setup():
        import jax, jax.numpy as jnp
        import numpy as np
        import math
        D = 128
        H = 16
        E = 8
        TOPK = 2
        LAT = D // 2
        KPH = LAT // H
        HD = D // H

        def _forward(hs, q_w, q_b, k_w, k_b, v_w, v_b, o_w, o_b, router_w, router_b, w1, b1, w2, b2):
            B, S, _ = hs.shape
            Q = (hs @ q_w + q_b).reshape(B, S, H, HD).transpose(0, 2, 1, 3)
            K = (hs @ k_w + k_b).reshape(B, S, H, KPH).transpose(0, 2, 1, 3)
            V = (hs @ v_w + v_b).reshape(B, S, H, KPH).transpose(0, 2, 1, 3)
            scores = jnp.einsum('bhsk,bhtk->bhst', Q[..., :KPH], K) / math.sqrt(KPH)
            attn = jax.nn.softmax(scores, axis=-1)
            ao = jnp.einsum('bhst,bhtv->bhsv', attn, V)
            ao = ao.transpose(0, 2, 1, 3).reshape(B, S, H * KPH)
            ao = jnp.concatenate([ao, jnp.zeros((B, S, D - LAT), ao.dtype)], axis=-1)
            mla_out = ao @ o_w + o_b
            probs = jax.nn.softmax(mla_out @ router_w + router_b, axis=-1)
            topw, topi = jax.lax.top_k(probs, TOPK)
            topw = topw / (topw.sum(-1, keepdims=True) + 1e-08)
            combine = jnp.sum(jax.nn.one_hot(topi, E, dtype=probs.dtype) * topw[..., None], axis=-2)
            h1 = jnp.einsum('bsd,edf->ebsf', mla_out, w1) + b1[:, None, None, :]
            h1 = jax.nn.gelu(h1, approximate=False)
            h2 = jnp.einsum('ebsf,efd->ebsd', h1, w2) + b2[:, None, None, :]
            moe_out = jnp.einsum('bse,ebsd->bsd', combine, h2)
            return hs + 0.3 * moe_out
        key = jax.random.key(seed)
        ks = jax.random.split(key, 16)
        s = 0.02
        inp = {'hidden_states': jax.random.normal(ks[0], (2, 256, D), jnp.float32), 'q_w': jax.random.normal(ks[1], (D, D), jnp.float32) * s, 'q_b': jnp.zeros((D,), jnp.float32), 'k_w': jax.random.normal(ks[2], (D, LAT), jnp.float32) * s, 'k_b': jnp.zeros((LAT,), jnp.float32), 'v_w': jax.random.normal(ks[3], (D, LAT), jnp.float32) * s, 'v_b': jnp.zeros((LAT,), jnp.float32), 'o_w': jax.random.normal(ks[4], (D, D), jnp.float32) * s, 'o_b': jnp.zeros((D,), jnp.float32), 'router_w': jax.random.normal(ks[5], (D, E), jnp.float32) * s, 'router_b': jnp.zeros((E,), jnp.float32), 'w1': jax.random.normal(ks[6], (E, D, 2 * D), jnp.float32) * s, 'b1': jnp.zeros((E, 2 * D), jnp.float32), 'w2': jax.random.normal(ks[7], (E, 2 * D, D), jnp.float32) * s, 'b2': jnp.zeros((E, D), jnp.float32)}
        return inp
    _L0_ffn_all = _L0_ffn_setup()
    _L0_ffn_in = {k: v for k, v in _L0_ffn_all.items() if k in ('q_w', 'q_b', 'k_w', 'k_b', 'v_w', 'v_b', 'o_w', 'o_b', 'router_w', 'router_b', 'w1', 'b1', 'w2', 'b2')}
    del _L0_ffn_all

    def _L1_attn_setup():
        import jax, jax.numpy as jnp
        import numpy as np
        D_MODEL = 128
        N_HEADS = 16
        KV_HEADS = 4
        D_HEAD = D_MODEL // N_HEADS

        def _rope_factor(n, d_head, dtype):
            i = jnp.arange(d_head)
            theta = jnp.power(jnp.asarray(10000.0, dtype), (-2.0 * (i // 2) / d_head).astype(dtype))
            pos = jnp.arange(n, dtype=dtype)
            ang = pos[:, None] * theta[None, :]
            sign = jnp.where(jnp.arange(n) % 2 == 1, -1.0, 1.0).astype(dtype)
            return jnp.cos(ang) + sign[:, None] * jnp.sin(ang)

        def _rms_norm(x, g):
            eps = jnp.finfo(x.dtype).eps
            inv = jax.lax.rsqrt(jnp.mean(x * x, axis=-1, keepdims=True) + eps)
            return x * inv * g
        key = jax.random.key(seed)
        ks = jax.random.split(key, 5)
        s_in = 1.0 / np.sqrt(D_MODEL)
        x = jax.random.normal(ks[0], (2, 256, D_MODEL), dtype=jnp.float32)
        w_q = jax.random.normal(ks[1], (D_MODEL, D_MODEL), dtype=jnp.float32) * s_in
        w_k = jax.random.normal(ks[2], (D_MODEL, D_HEAD * KV_HEADS), dtype=jnp.float32) * s_in
        w_v = jax.random.normal(ks[3], (D_MODEL, D_HEAD * KV_HEADS), dtype=jnp.float32) * s_in
        w_o = jax.random.normal(ks[4], (D_MODEL, D_MODEL), dtype=jnp.float32) * s_in
        g = jnp.ones((D_MODEL,), dtype=jnp.float32)
        return {'x': x, 'w_q': w_q, 'w_k': w_k, 'w_v': w_v, 'w_o': w_o, 'g': g}
    _L1_attn_all = _L1_attn_setup()
    _L1_attn_in = {k: v for k, v in _L1_attn_all.items() if k in ('w_q', 'w_k', 'w_v', 'w_o', 'g')}
    del _L1_attn_all

    def _L1_xattn_setup():
        import jax, jax.numpy as jnp
        import numpy as np
        D_MODEL = 128
        NHEAD = 16
        NUM_KV = 4
        D_K = D_MODEL // NHEAD
        GROUP = NHEAD // NUM_KV
        ROPE_BASE = 10000.0

        def _rope(x, seq_len):
            half = D_K // 2
            inv_freq = 1.0 / ROPE_BASE ** (jnp.arange(0, D_K, 2, dtype=jnp.float32) / D_K)
            t = jnp.arange(seq_len, dtype=jnp.float32)
            freqs = jnp.outer(t, inv_freq)
            emb = jnp.concatenate([freqs, freqs], axis=-1)
            cos, sin = (jnp.cos(emb), jnp.sin(emb))
            x1, x2 = (x[..., :half], x[..., half:])
            rot = jnp.concatenate([-x2, x1], axis=-1)
            return x * cos + rot * sin
        key = jax.random.key(seed)
        ks = jax.random.split(key, 12)
        B, S = (2, 256)
        s_in = 1.0 / np.sqrt(D_MODEL)
        inp = {'query': jax.random.normal(ks[0], (B, S, D_MODEL), jnp.float32), 'key': jax.random.normal(ks[1], (B, S, D_MODEL), jnp.float32), 'value': jax.random.normal(ks[2], (B, S, D_MODEL), jnp.float32), 'Wq': jax.random.normal(ks[3], (D_MODEL, D_MODEL), jnp.float32) * s_in, 'bq': jnp.zeros((D_MODEL,), jnp.float32), 'Wk': jax.random.normal(ks[4], (NUM_KV * D_K, D_MODEL), jnp.float32) * s_in, 'bk': jnp.zeros((NUM_KV * D_K,), jnp.float32), 'Wv': jax.random.normal(ks[5], (NUM_KV * D_K, D_MODEL), jnp.float32) * s_in, 'bv': jnp.zeros((NUM_KV * D_K,), jnp.float32), 'Wo': jax.random.normal(ks[6], (D_MODEL, D_MODEL), jnp.float32) * s_in, 'bo': jnp.zeros((D_MODEL,), jnp.float32)}
        return inp
    _L1_xattn_all = _L1_xattn_setup()
    _L1_xattn_in = {k: v for k, v in _L1_xattn_all.items() if k in ('Wq', 'bq', 'Wk', 'bk', 'Wv', 'bv', 'Wo', 'bo')}
    del _L1_xattn_all

    def _L1_ffn_setup():
        import jax, jax.numpy as jnp
        import numpy as np
        N_EMBD = 128
        N_STATE = 512
        key = jax.random.key(seed)
        k_x, k_w1, k_b1, k_w2, k_b2 = jax.random.split(key, 5)
        x = jax.random.normal(k_x, (4, 256, N_EMBD), dtype=jnp.float32)
        w1 = jax.random.normal(k_w1, (N_EMBD, N_STATE), dtype=jnp.float32) * (1.0 / np.sqrt(N_EMBD))
        b1 = jax.random.normal(k_b1, (N_STATE,), dtype=jnp.float32) * 0.02
        w2 = jax.random.normal(k_w2, (N_STATE, N_EMBD), dtype=jnp.float32) * (1.0 / np.sqrt(N_STATE))
        b2 = jax.random.normal(k_b2, (N_EMBD,), dtype=jnp.float32) * 0.02
        return {'x': x, 'w1': w1, 'b1': b1, 'w2': w2, 'b2': b2}
    _L1_ffn_all = _L1_ffn_setup()
    _L1_ffn_in = {k: v for k, v in _L1_ffn_all.items() if k in ('w1', 'b1', 'w2', 'b2')}
    del _L1_ffn_all
    return {'x': x, 'ctx_1024': ctx_1024, 'L0_attn_A_log': _L0_attn_in['A_log'], 'L0_attn_W_B': _L0_attn_in['W_B'], 'L0_attn_W_C': _L0_attn_in['W_C'], 'L0_attn_D_skip': _L0_attn_in['D_skip'], 'L0_attn_log_dt': _L0_attn_in['log_dt'], 'L0_attn_W_in': _L0_attn_in['W_in'], 'L0_attn_b_in': _L0_attn_in['b_in'], 'L0_attn_W_out': _L0_attn_in['W_out'], 'L0_attn_b_out': _L0_attn_in['b_out'], 'L0_attn_ln_g': _L0_attn_in['ln_g'], 'L0_attn_ln_b': _L0_attn_in['ln_b'], 'L0_xattn_w_q': _L0_xattn_in['w_q'], 'L0_xattn_w_k': _L0_xattn_in['w_k'], 'L0_xattn_w_v': _L0_xattn_in['w_v'], 'L0_xattn_w_o': _L0_xattn_in['w_o'], 'L0_xattn_b_q': _L0_xattn_in['b_q'], 'L0_xattn_b_k': _L0_xattn_in['b_k'], 'L0_xattn_b_v': _L0_xattn_in['b_v'], 'L0_xattn_b_o': _L0_xattn_in['b_o'], 'L0_ffn_q_w': _L0_ffn_in['q_w'], 'L0_ffn_q_b': _L0_ffn_in['q_b'], 'L0_ffn_k_w': _L0_ffn_in['k_w'], 'L0_ffn_k_b': _L0_ffn_in['k_b'], 'L0_ffn_v_w': _L0_ffn_in['v_w'], 'L0_ffn_v_b': _L0_ffn_in['v_b'], 'L0_ffn_o_w': _L0_ffn_in['o_w'], 'L0_ffn_o_b': _L0_ffn_in['o_b'], 'L0_ffn_router_w': _L0_ffn_in['router_w'], 'L0_ffn_router_b': _L0_ffn_in['router_b'], 'L0_ffn_w1': _L0_ffn_in['w1'], 'L0_ffn_b1': _L0_ffn_in['b1'], 'L0_ffn_w2': _L0_ffn_in['w2'], 'L0_ffn_b2': _L0_ffn_in['b2'], 'L1_attn_w_q': _L1_attn_in['w_q'], 'L1_attn_w_k': _L1_attn_in['w_k'], 'L1_attn_w_v': _L1_attn_in['w_v'], 'L1_attn_w_o': _L1_attn_in['w_o'], 'L1_attn_g': _L1_attn_in['g'], 'L1_xattn_Wq': _L1_xattn_in['Wq'], 'L1_xattn_bq': _L1_xattn_in['bq'], 'L1_xattn_Wk': _L1_xattn_in['Wk'], 'L1_xattn_bk': _L1_xattn_in['bk'], 'L1_xattn_Wv': _L1_xattn_in['Wv'], 'L1_xattn_bv': _L1_xattn_in['bv'], 'L1_xattn_Wo': _L1_xattn_in['Wo'], 'L1_xattn_bo': _L1_xattn_in['bo'], 'L1_ffn_w1': _L1_ffn_in['w1'], 'L1_ffn_b1': _L1_ffn_in['b1'], 'L1_ffn_w2': _L1_ffn_in['w2'], 'L1_ffn_b2': _L1_ffn_in['b2']}

def reference(x, ctx_1024, L0_attn_A_log, L0_attn_W_B, L0_attn_W_C, L0_attn_D_skip, L0_attn_log_dt, L0_attn_W_in, L0_attn_b_in, L0_attn_W_out, L0_attn_b_out, L0_attn_ln_g, L0_attn_ln_b, L0_xattn_w_q, L0_xattn_w_k, L0_xattn_w_v, L0_xattn_w_o, L0_xattn_b_q, L0_xattn_b_k, L0_xattn_b_v, L0_xattn_b_o, L0_ffn_q_w, L0_ffn_q_b, L0_ffn_k_w, L0_ffn_k_b, L0_ffn_v_w, L0_ffn_v_b, L0_ffn_o_w, L0_ffn_o_b, L0_ffn_router_w, L0_ffn_router_b, L0_ffn_w1, L0_ffn_b1, L0_ffn_w2, L0_ffn_b2, L1_attn_w_q, L1_attn_w_k, L1_attn_w_v, L1_attn_w_o, L1_attn_g, L1_xattn_Wq, L1_xattn_bq, L1_xattn_Wk, L1_xattn_bk, L1_xattn_Wv, L1_xattn_bv, L1_xattn_Wo, L1_xattn_bo, L1_ffn_w1, L1_ffn_b1, L1_ffn_w2, L1_ffn_b2):
    import jax
    import jax.numpy as jnp

    def _L0_attn_ref(x, A_log, W_B, W_C, D_skip, log_dt, W_in, b_in, W_out, b_out, ln_g, ln_b):
        import jax, jax.numpy as jnp
        import numpy as np
        B, L, D, S = (4, 256, 128, 16)
        Bb, Ll, Dd = x.shape
        residual = x
        mu = x.mean(-1, keepdims=True)
        var = ((x - mu) ** 2).mean(-1, keepdims=True)
        xn = (x - mu) / jnp.sqrt(var + 1e-05) * ln_g + ln_b
        xz = xn @ W_in.T + b_in
        x_proj, z = jnp.split(xz, 2, axis=-1)
        z = jax.nn.silu(z)
        dt = jnp.clip(jnp.exp(log_dt), 0.0001, 1.0)
        A_bar = jnp.exp(-jnp.exp(A_log) * dt[:, None])
        A_bar = jnp.clip(A_bar, 1e-08, 1.0 - 1e-08)
        B_proj = x_proj @ W_B.T * dt.mean()
        t_idx = jnp.arange(Ll, dtype=jnp.float32)
        log_A = jnp.log(A_bar)
        A_mean = jnp.exp(t_idx[:, None, None] * log_A[None]).mean(axis=1)
        kernel = jnp.flip(A_mean.T, -1)[:, None, :]
        lhs = jnp.transpose(B_proj, (0, 2, 1))
        x_mean = jax.lax.conv_general_dilated(lhs, kernel, window_strides=(1,), padding=((Ll - 1, 0),), dimension_numbers=('NCH', 'OIH', 'NCH'), feature_group_count=kernel.shape[0])
        x_mean = jnp.transpose(x_mean, (0, 2, 1))
        y = x_mean @ W_C.T + D_skip * x_proj
        y = y * z
        y = y @ W_out.T + b_out
        return y + residual

    def _L0_xattn_ref(query, key, value, w_q, w_k, w_v, w_o, b_q, b_k, b_v, b_o):
        import jax, jax.numpy as jnp
        import numpy as np
        D_MODEL = 128
        N_HEADS = 16
        D_K = D_MODEL // N_HEADS

        def _xavier(key, shape):
            fan_in, fan_out = (shape[1], shape[0])
            a = float(np.sqrt(6.0 / (fan_in + fan_out)))
            return jax.random.uniform(key, shape, jnp.float32, -a, a)
        B = query.shape[0]
        scale = jnp.sqrt(jnp.asarray(D_K, query.dtype))

        def split_heads(x):
            return x.reshape(B, -1, N_HEADS, D_K).transpose(0, 2, 1, 3)
        q = split_heads(query @ w_q.T + b_q)
        k = split_heads(key @ w_k.T + b_k)
        v = split_heads(value @ w_v.T + b_v)
        scores = jnp.einsum('bhqd,bhkd->bhqk', q, k) / scale
        attn = jax.nn.softmax(scores, axis=-1)
        ctx = jnp.einsum('bhqk,bhkd->bhqd', attn, v)
        ctx = ctx.transpose(0, 2, 1, 3).reshape(B, -1, D_MODEL)
        out = ctx @ w_o.T + b_o
        return out

    def _L0_ffn_ref(hidden_states, q_w, q_b, k_w, k_b, v_w, v_b, o_w, o_b, router_w, router_b, w1, b1, w2, b2):
        import jax, jax.numpy as jnp
        import numpy as np
        import math
        D = 128
        H = 16
        E = 8
        TOPK = 2
        LAT = D // 2
        KPH = LAT // H
        HD = D // H

        def _forward(hs, q_w, q_b, k_w, k_b, v_w, v_b, o_w, o_b, router_w, router_b, w1, b1, w2, b2):
            B, S, _ = hs.shape
            Q = (hs @ q_w + q_b).reshape(B, S, H, HD).transpose(0, 2, 1, 3)
            K = (hs @ k_w + k_b).reshape(B, S, H, KPH).transpose(0, 2, 1, 3)
            V = (hs @ v_w + v_b).reshape(B, S, H, KPH).transpose(0, 2, 1, 3)
            scores = jnp.einsum('bhsk,bhtk->bhst', Q[..., :KPH], K) / math.sqrt(KPH)
            attn = jax.nn.softmax(scores, axis=-1)
            ao = jnp.einsum('bhst,bhtv->bhsv', attn, V)
            ao = ao.transpose(0, 2, 1, 3).reshape(B, S, H * KPH)
            ao = jnp.concatenate([ao, jnp.zeros((B, S, D - LAT), ao.dtype)], axis=-1)
            mla_out = ao @ o_w + o_b
            probs = jax.nn.softmax(mla_out @ router_w + router_b, axis=-1)
            topw, topi = jax.lax.top_k(probs, TOPK)
            topw = topw / (topw.sum(-1, keepdims=True) + 1e-08)
            combine = jnp.sum(jax.nn.one_hot(topi, E, dtype=probs.dtype) * topw[..., None], axis=-2)
            h1 = jnp.einsum('bsd,edf->ebsf', mla_out, w1) + b1[:, None, None, :]
            h1 = jax.nn.gelu(h1, approximate=False)
            h2 = jnp.einsum('ebsf,efd->ebsd', h1, w2) + b2[:, None, None, :]
            moe_out = jnp.einsum('bse,ebsd->bsd', combine, h2)
            return hs + 0.3 * moe_out
        return _forward(hidden_states, q_w, q_b, k_w, k_b, v_w, v_b, o_w, o_b, router_w, router_b, w1, b1, w2, b2)

    def _L1_attn_ref(x, w_q, w_k, w_v, w_o, g):
        import jax, jax.numpy as jnp
        import numpy as np
        D_MODEL = 128
        N_HEADS = 16
        KV_HEADS = 4
        D_HEAD = D_MODEL // N_HEADS

        def _rope_factor(n, d_head, dtype):
            i = jnp.arange(d_head)
            theta = jnp.power(jnp.asarray(10000.0, dtype), (-2.0 * (i // 2) / d_head).astype(dtype))
            pos = jnp.arange(n, dtype=dtype)
            ang = pos[:, None] * theta[None, :]
            sign = jnp.where(jnp.arange(n) % 2 == 1, -1.0, 1.0).astype(dtype)
            return jnp.cos(ang) + sign[:, None] * jnp.sin(ang)

        def _rms_norm(x, g):
            eps = jnp.finfo(x.dtype).eps
            inv = jax.lax.rsqrt(jnp.mean(x * x, axis=-1, keepdims=True) + eps)
            return x * inv * g
        b, n, _ = x.shape
        reps = N_HEADS // KV_HEADS
        x_norm = _rms_norm(x, g)
        q = (x_norm @ w_q).reshape(b, n, N_HEADS, D_HEAD).transpose(0, 2, 1, 3)
        k = (x_norm @ w_k).reshape(b, n, KV_HEADS, D_HEAD).transpose(0, 2, 1, 3)
        v = (x_norm @ w_v).reshape(b, n, KV_HEADS, D_HEAD).transpose(0, 2, 1, 3)
        rf = _rope_factor(n, D_HEAD, x.dtype)
        q = q * rf
        k = k * rf
        q5 = q.reshape(b, reps, KV_HEADS, n, D_HEAD)
        scale = jnp.asarray(np.sqrt(D_MODEL), x.dtype)
        qkt = jnp.einsum('brkqa,bkca->brkqc', q5, k) / scale
        attn = jax.nn.softmax(qkt, axis=-1)
        s = jnp.einsum('brkqc,bkca->brkqa', attn, v)
        s = s.reshape(b, N_HEADS, n, D_HEAD).transpose(0, 2, 1, 3).reshape(b, n, D_MODEL)
        o = s @ w_o
        return s + o

    def _L1_xattn_ref(query, key, value, Wq, bq, Wk, bk, Wv, bv, Wo, bo):
        import jax, jax.numpy as jnp
        import numpy as np
        D_MODEL = 128
        NHEAD = 16
        NUM_KV = 4
        D_K = D_MODEL // NHEAD
        GROUP = NHEAD // NUM_KV
        ROPE_BASE = 10000.0

        def _rope(x, seq_len):
            half = D_K // 2
            inv_freq = 1.0 / ROPE_BASE ** (jnp.arange(0, D_K, 2, dtype=jnp.float32) / D_K)
            t = jnp.arange(seq_len, dtype=jnp.float32)
            freqs = jnp.outer(t, inv_freq)
            emb = jnp.concatenate([freqs, freqs], axis=-1)
            cos, sin = (jnp.cos(emb), jnp.sin(emb))
            x1, x2 = (x[..., :half], x[..., half:])
            rot = jnp.concatenate([-x2, x1], axis=-1)
            return x * cos + rot * sin
        B, S, _ = query.shape
        T = key.shape[1]
        Q = (query @ Wq.T + bq).reshape(B, S, NHEAD, D_K).transpose(0, 2, 1, 3)
        K = (key @ Wk.T + bk).reshape(B, T, NUM_KV, D_K).transpose(0, 2, 1, 3)
        V = (value @ Wv.T + bv).reshape(B, T, NUM_KV, D_K).transpose(0, 2, 1, 3)
        Q = _rope(Q, S)
        K = _rope(K, T)
        Kr = jnp.repeat(K, GROUP, axis=1)
        Vr = jnp.repeat(V, GROUP, axis=1)
        scale = 1.0 / np.sqrt(D_K)
        scores = jnp.einsum('bhsd,bhtd->bhst', Q, Kr) * scale
        attn = jax.nn.softmax(scores, axis=-1)
        context = jnp.einsum('bhst,bhtd->bhsd', attn, Vr)
        context = context.transpose(0, 2, 1, 3).reshape(B, S, D_MODEL)
        return context @ Wo.T + bo

    def _L1_ffn_ref(x, w1, b1, w2, b2):
        import jax, jax.numpy as jnp
        import numpy as np
        N_EMBD = 128
        N_STATE = 512
        h = jax.nn.gelu(jnp.einsum('bse,eh->bsh', x, w1) + b1, approximate=False)
        return jnp.einsum('bsh,he->bse', h, w2) + b2
    x = x + _L0_attn_ref(_layernorm(x, axis=-1), L0_attn_A_log, L0_attn_W_B, L0_attn_W_C, L0_attn_D_skip, L0_attn_log_dt, L0_attn_W_in, L0_attn_b_in, L0_attn_W_out, L0_attn_b_out, L0_attn_ln_g, L0_attn_ln_b)
    x = x + _L0_xattn_ref(_layernorm(x, axis=-1), ctx_1024, ctx_1024, L0_xattn_w_q, L0_xattn_w_k, L0_xattn_w_v, L0_xattn_w_o, L0_xattn_b_q, L0_xattn_b_k, L0_xattn_b_v, L0_xattn_b_o)
    x = x + _L0_ffn_ref(_layernorm(x, axis=-1), L0_ffn_q_w, L0_ffn_q_b, L0_ffn_k_w, L0_ffn_k_b, L0_ffn_v_w, L0_ffn_v_b, L0_ffn_o_w, L0_ffn_o_b, L0_ffn_router_w, L0_ffn_router_b, L0_ffn_w1, L0_ffn_b1, L0_ffn_w2, L0_ffn_b2)
    x = x + _L1_attn_ref(_layernorm(x, axis=-1), L1_attn_w_q, L1_attn_w_k, L1_attn_w_v, L1_attn_w_o, L1_attn_g)
    x = x + _L1_xattn_ref(_layernorm(x, axis=-1), ctx_1024, ctx_1024, L1_xattn_Wq, L1_xattn_bq, L1_xattn_Wk, L1_xattn_bk, L1_xattn_Wv, L1_xattn_bv, L1_xattn_Wo, L1_xattn_bo)
    x = x + _L1_ffn_ref(_layernorm(x, axis=-1), L1_ffn_w1, L1_ffn_b1, L1_ffn_w2, L1_ffn_b2)
    return x

_drawn_inputs = setup_inputs


def setup_inputs(seed=0):
    import zlib

    import numpy as np

    out = dict(_drawn_inputs(seed))
    spreads = {'L0_attn_D_skip': (1.0, 0.6),
     'L0_attn_ln_g': (1.0, 0.6),
     'L0_attn_ln_b': (0.0, 0.8),
     'L0_xattn_b_q': (0.0, 0.662),
     'L0_xattn_b_k': (0.0, 2.0),
     'L0_xattn_b_v': (0.0, 0.1),
     'L0_xattn_b_o': (0.0, 0.1),
     'L0_ffn_q_b': (0.0, 0.8),
     'L0_ffn_k_b': (0.0, 2.0),
     'L0_ffn_v_b': (0.0, 0.8),
     'L0_ffn_o_b': (0.0, 0.8),
     'L0_ffn_router_b': (0.0, 0.8),
     'L0_ffn_b1': (0.0, 0.8),
     'L0_ffn_b2': (0.0, 0.8),
     'L1_attn_g': (1.0, 0.6),
     'L1_xattn_bq': (0.0, 0.8),
     'L1_xattn_bk': (0.0, 2.0),
     'L1_xattn_bv': (0.0, 0.293),
     'L1_xattn_bo': (0.0, 0.337)}
    factors = {'L0_attn_A_log': 8.0,
     'L0_attn_W_B': 8.0,
     'L0_attn_W_C': 8.0,
     'L0_attn_log_dt': 8.0,
     'L0_attn_b_in': 7.581,
     'L0_ffn_q_w': 8.0,
     'L0_ffn_k_w': 8.0,
     'L0_ffn_v_w': 8.0,
     'L0_ffn_o_w': 8.0,
     'L0_ffn_router_w': 8.0,
     'L0_ffn_w1': 8.0,
     'L0_ffn_w2': 8.0,
     'L1_attn_w_q': 6.201,
     'L1_attn_w_k': 6.404,
     'L1_ffn_b1': 8.0,
     'L1_ffn_b2': 8.0}
    for name, (base, spread) in spreads.items():
        noise = np.random.default_rng([zlib.crc32(name.encode()), seed]).standard_normal(out[name].shape)
        drawn = base * np.exp(spread * noise) if base else spread * noise
        out[name] = jnp.asarray(drawn.astype(out[name].dtype))
    for name, factor in factors.items():
        out[name] = (out[name] * factor).astype(out[name].dtype)
    return out
```

```python
from contextlib import ExitStack

import numpy as np

import concourse.bass as bass
import concourse.mybir as mybir

F32 = mybir.dt.float32
BF16 = mybir.dt.bfloat16
ALU = mybir.AluOpType
ACT = mybir.ActivationFunctionType
AX = mybir.AxisListType

B, S, D, C = 8, 256, 128, 64
T = S // 128
PAIRS = B // 2
H = 16
NS = 16
E = 8
MS = 2
DEN = 8
LN_EPS = 1e-5
RMS_EPS = float(np.finfo(np.float32).eps)

LAYERS = {
    "x0": dict(d=8, W=64, HB=2, KG=8, scale=8.0 ** -0.5, cross=True),
    "s0": dict(d=4, W=32, HB=4, KG=4, scale=0.5, cross=False),
    "s1": dict(d=8, W=64, HB=2, KG=2, scale=128.0 ** -0.5, cross=False),
    "x1": dict(d=8, W=64, HB=2, KG=4, scale=8.0 ** -0.5, cross=True),
}
Q_PARTS = ((0, 1, 3), (3, 2, 2), (4, 1, 1))
K_PARTS = ((2, 1, 3), (0, 5, 2), (1, 1, 1))

A_BANKS, B_BANKS, P_SLOTS = 2, 2, 4

W_COLS = [("win", 256), ("wb", 16), ("wout", 128),
          ("x0q", 128), ("x0k", 128), ("x0v", 128), ("x0o", 128),
          ("x1q", 128), ("x1k", 32), ("x1v", 32), ("x1o", 128),
          ("s0qk", 128), ("s0v", 64), ("s0o", 128), ("router", 8),
          ("s1qk", 160), ("s1v", 32), ("s1o", 128),
          ("ident", 128), ("ones", 128),
          ("bx", 1), ("bz", 1), ("dskip", 1), ("lng", 1), ("lnb", 1), ("rmsg", 1), ("mlab", 1),
          ("logdt", 1), ("alog", NS), ("b1", 16), ("fb1", 4)]
R_COLS = [("bout", 128), ("x0bq", 256), ("x0bk", 128), ("x0bv", 128), ("x0bo", 128),
          ("x1bq", 256), ("x1bk", 32), ("x1bv", 32), ("x1bo", 128),
          ("s0bq", 128), ("s0bk", 128), ("s0bv", 128), ("rb", 16), ("fb2", 128),
          ("tri", 128), ("iota", 256)]
T_COLS = [("rf", 16), ("qcos", 16), ("qsin", 16), ("kcos", 8), ("ksin", 8)]


def columns(table):
    at, out = 0, {}
    for name, width in table:
        out[name] = (at, at + width)
        at += width
    return out, at


W_AT, W_N = columns(W_COLS)
R_AT, R_N = columns(R_COLS)
T_AT, T_N = columns(T_COLS)


class Step:

    def __init__(self, kind, L=None, j=0, q=0):
        self.kind, self.L, self.j, self.q = kind, L, j, q


def stream(j):
    out = [Step(k, "m", j) for k in ("T1", "T2", "T3", "T4", "T5", "T6")]

    def attention(L):
        out.extend([Step("P1", L, j), Step("P2", L, j), Step("P3", L, j)])
        out.extend(Step("A", L, j, q) for q in range(4))
        out.append(Step("N", L, j))
        n = 4 if LAYERS[L]["cross"] else 8
        out.extend(Step(k, L, j, q) for i in range(n + 1) for k, q in (("S", i), ("V", i - 1)) if 0 <= q < n)
        out.extend([Step("F1", L, j), Step("F2", L, j), Step("F3", L, j)])

    attention("x0")
    attention("s0")
    out.append(Step("R1", "s0", j))
    out.append(Step("G", "s0", j, 0))
    out.append(Step("R2", "s0", j))
    for e in range(1, E):
        out.append(Step("G", "s0", j, e))
        out.append(Step("H", "s0", j, e - 1))
    out.append(Step("H", "s0", j, E - 1))
    attention("s1")
    attention("x1")
    out.extend([Step("P1", "f", j), Step("G", "f", j, 0), Step("G", "f", j, 1), Step("H", "f", j, 0)])
    return out


ORDER = (
    "00c001c1001010101100100001000011000110010111011101111011010010011010100100000000"
    "01101101101011111011111010101101001011001010101100101101001101010101000001101010"
    "01000000000001001011011110111111110110110100001001101001000101101111011110101011"
    "01")


def schedule():
    todo = {"0": stream(0), "1": stream(1), "c": [Step("C", "x0"), Step("C", "x1")]}
    return [todo[n].pop(0) for n in ORDER if todo[n]]


def misc_names(s):
    L = LAYERS.get(s.L, {})
    groups = H // L["HB"] if L else 0
    halves = max(groups // 4, 1)
    if s.kind == "P3":
        return ([] if L["cross"] else ["k"]) + [f"q{n}" for n in range(halves)]
    if s.kind == "N":
        return [f"q{n}" for n in range(halves)]
    if s.kind == "C":
        return ["kv", "kT"]
    if s.kind == "R2":
        return ["cT", "cb"]
    if s.kind in ("T1", "T2", "T3", "T4", "T5", "T6", "P1", "P2", "F1", "F2", "F3", "R1"):
        return ["m"]
    return []


def units(s):
    cross = s.L in LAYERS and LAYERS[s.L]["cross"]
    if s.kind == "A":
        return (1 if cross else 4), 0
    if s.kind == "S":
        return 0, (1 if cross else 2)
    if s.kind == "G":
        return 0, 1
    if s.kind == "H":
        return 1, 0
    return 0, 0


def marks(s):
    out = {}
    cross = s.L in LAYERS and LAYERS[s.L]["cross"]
    if s.kind in ("T1", "P1"):
        twice = 2 if s.kind == "T1" or s.L == "s1" else 1
        out.update(stats_ready=twice, rstd_ready=twice, xn_ready=1)
    if s.kind == "P2" and s.L == "x1":
        out["qk_ready"] = 1
    if s.kind == "C" and s.L == "x1":
        out["qk_ready"] = 1
    if s.kind in ("P3", "C"):
        out["split_done"] = 1
    if s.kind == "P3" and not cross:
        out[f"qblk_loaded{s.j}"] = 64
    if s.kind == "N":
        out["max_in_slots"] = 1
        if not cross:
            out[f"mrow_loaded{s.j}"] = 64
    if s.kind == "T5":
        out["y_ready"] = 1
    if s.kind in ("T6", "F3", "R2") or (s.kind == "H" and s.L == "f"):
        if not (s.kind == "F3" and s.L == "s0"):
            out["base_ready"] = 1
    if s.kind == "F1":
        out[f"ot_drained{s.j}"] = 1
    if s.kind == "V":
        out["p_used"] = 1 if cross else 2
    if s.kind == "R1":
        out.update(logits_ready=1, router_exp=1, gates_ready=1)
    if s.kind == "H" and s.L == "f":
        out["stored"] = 16
    return out


def number(steps):
    k = a = b = 0
    total, per_bank, slots = {}, [0, 0], [0, 0]
    for s in steps:
        s.misc = {}
        for name in misc_names(s):
            bank = k % 2
            per_bank[bank] += 1
            s.misc[name] = (bank, per_bank[bank])
            k += 1
        na, nb = units(s)
        s.a, s.b = a, b
        a += na
        b += nb
        s.p = [s.j * P_SLOTS + (slots[s.j] + n) % P_SLOTS for n in range(nb)]
        slots[s.j] += nb
        for name, n in marks(s).items():
            total[name] = total.get(name, 0) + n
        s.after = dict(total)
    used = []
    for s in steps:
        if s.kind == "S":
            v = next(x for x in steps if (x.kind, x.L, x.j, x.q) == ("V", s.L, s.j, s.q))
            used += [(p, "p_used", v.after["p_used"]) for p in s.p]
        if s.kind == "G":
            h = next(x for x in steps if (x.kind, x.L, x.j, x.q) == ("H", s.L, s.j, s.q if s.L == "s0" else 0))
            used += [(p, "a_filled", h.a + 1) for p in s.p]
    assert len(used) == b
    total.update(a_filled=a, a_drained=a, b_filled=b, b_drained=b)
    for m in range(2):
        total[f"misc_filled{m}"] = total[f"misc_drained{m}"] = per_bank[m]
    release = {}
    for unit, (p, _, _) in enumerate(used):
        before = [u for u in range(unit) if used[u][0] == p]
        last = before[-1] if before else max(u for u in range(b) if used[u][0] == p)
        _, name, n = used[last]
        release[unit] = (name, n if before else n - total[name])
    return total, release


DVE_STEPS, POOL_STEPS = 179, 72


def decoder(nc, x_in, ctx_in, w_in, w1_in, w2_in, b2_in, fw1_in, fw2_in, wc_in, rows_in, rope_in, flip_in, out):
    steps = schedule()
    total, p_release = number(steps)
    total.update(dve_step=DVE_STEPS, pool_step=POOL_STEPS, x_loaded0=16, x_loaded1=16, ctx_loaded=48)
    PRIME = dict(a_drained=A_BANKS, b_drained=B_BANKS, p_used=total["p_used"], a_filled=total["a_filled"], misc_drained0=1, misc_drained1=1,
                 ot_drained0=1, ot_drained1=1, stored=16)

    with ExitStack() as ctx:
        def sb(name, shape, dt=F32):
            return ctx.enter_context(nc.sbuf_tensor(name, shape, dt))

        def both(name, shape, dt=F32):
            return [sb(f"{name}{j}", shape, dt) for j in range(2)]

        def sem(name):
            return ctx.enter_context(nc.semaphore(name))

        W = sb("W", [128, W_N])
        w1 = sb("w1", [128, E * 2 * 128])
        w2 = sb("w2", [128, E * 2 * D])
        fw1 = sb("fw1", [128, 512])
        fw2 = sb("fw2", [128, 4 * D])
        b2 = sb("b2", [128, D])
        wc = sb("wc", [128, D])
        rows = sb("rows", [128, R_N])
        rope = sb("rope", [128, T_N])
        identb = sb("identb", [128, 128], BF16)
        minus_half = sb("minus_half", [128, T])
        zero = sb("zero", [128, 1])
        wait_carrier = sb("wait_carrier", [128, 1])
        ln_eps = sb("ln_eps", [128, T])
        rms_eps = sb("rms_eps", [128, T])
        dt = sb("dt", [128, 8])
        tokens = sb("tokens", [128, 9])
        toep = sb("toep", [128, NS, S])

        x = both("x", [128, T, D])
        base = both("base", [128, T, D])
        xn = both("xn", [128, T, D])
        xn2 = both("xn2", [128, T, D])
        xnT = both("xnT", [128, S])
        stats = both("stats", [128, T, 6])
        mv = both("mv", [128, T, 2])
        ms = both("ms", [128, T])
        veps = both("veps", [128, T])
        rstd = both("rstd", [128, T])
        xpT = both("xpT", [128, S])
        zs = both("zs", [128, S])
        bdiag = [sb("bdiag", [128, T, NS * 32 + 32])] * 2
        xm = both("xm", [128, S])
        y1 = both("y1", [128, S])
        y2 = both("y2", [128, S])
        qf = both("qf", [128, T, 128])
        qt1 = [y1[j][:, :].rearrange("p (t c) -> p t c", t=T) for j in range(2)]
        qt2 = [y2[j][:, :].rearrange("p (t c) -> p t c", t=T) for j in range(2)]
        kf = both("kf", [128, T, 64])
        qres = [sb("qres", [128, 256])] * 2
        qs = {32: both("qs32_", [128, T * H, 32], BF16), 64: both("qs64_", [128, T * H, 64], BF16)}
        ks = {"s0": both("ks_s0", [128, T * H, 32], BF16), "s1": both("ks_s1", [128, T * 4, 64], BF16)}
        QT = both("QT", [128, 8, S], BF16)
        QM = QT
        KT = both("KT", [128, 4, S], BF16)
        qblk = {"s0": both("qblk_s0", [128, H, S], BF16), "s1": both("qblk_s1", [128, H, S], BF16)}
        vp = {"s0": both("vp_s0", [128, T * H * 32 + 160]), "s1": both("vp_s1", [128, T * 8 * 32 + 160])}
        nmax = both("nmax", [128, T, H])
        ots = both("ots", [128, 2, S])
        rden = both("rden", [128, 32])
        on = both("on", [128, T, D])
        on4 = both("on4", [128, T, D])
        onT = xpT
        mlaT = xm
        lg = both("lg", [128, T, E])
        lmax = both("lmax", [128, T])
        lexp = both("lexp", [128, T, E])
        gsum = both("gsum", [128, T])
        prob = both("prob", [128, T * E])
        above = [y1[j][:, 0:T * E * E] for j in range(2)]
        ties = [y1[j][:, T * E * E:2 * T * E * E] for j in range(2)]
        rank = both("rank", [128, T * E])
        gate = both("gate", [128, T, 128])
        gateT = zs
        yout = both("yout", [128, T, D])
        ctxk = sb("ctxk", [128, 2, C])
        ctxp = sb("ctxp", [128, 2, 2, C])
        ckf = sb("ckf", [128, 128])
        ck1 = sb("ck1", [128, 32])
        ck2 = sb("ck2", [128, 32])
        ck3 = sb("ck3", [128, 32])
        cres = sb("cres", [128, 128])
        kx = {"x0": sb("kx0", [128, 16, 64], BF16), "x1": sb("kx1", [128, 8, 64], BF16)}
        kblk = {"x0": both("kblk0", [128, 8, 128], BF16), "x1": both("kblk1", [128, 4, 128], BF16)}
        vx = {"x0": both("vx0", [128, 8, 32]), "x1": both("vx1", [128, 8, 32])}
        P = sb("P", [128, 2 * P_SLOTS, 2, S])

        psA = ctx.enter_context(nc.psum_tensor("psA", [128, A_BANKS, 512], F32))
        psB = ctx.enter_context(nc.psum_tensor("psB", [128, B_BANKS, 512], F32))
        psO = ctx.enter_context(nc.psum_tensor("psO", [128, 2, 2, S], F32))
        psM = ctx.enter_context(nc.psum_tensor("psM", [128, 2, 512], F32))
        decay = nc.dram_tensor("decay_rows", [NS, 128 + S], F32, kind="Internal").ap()

        names = ["a_filled", "a_drained", "b_filled", "b_drained", "p_used",
                 "stats_ready", "rstd_ready", "xn_ready", "qk_ready", "split_done", "max_in_slots", "y_ready", "base_ready",
                 "logits_ready", "router_exp", "gates_ready", "stored", "ctx_loaded", "dve_step", "pool_step"]
        sems = {n: sem(n) for n in names}
        (a_filled, a_drained, b_filled, b_drained, p_used, stats_ready, rstd_ready, xn_ready, qk_ready,
         split_done, max_in_slots, y_ready, base_ready,
         logits_ready, router_exp, gates_ready, stored, ctx_loaded,
         dve_step, pool_step) = (sems[n] for n in names)
        misc_filled = [sem(f"misc_filled{m}") for m in range(2)]
        misc_drained = [sem(f"misc_drained{m}") for m in range(2)]
        x_loaded = [sem(f"x_loaded{j}") for j in range(2)]
        ot_drained = [sem(f"ot_drained{j}") for j in range(2)]
        qblk_loaded = [sem(f"qblk_loaded{j}") for j in range(2)]
        mrow_loaded = [sem(f"mrow_loaded{j}") for j in range(2)]
        weights_loaded = sem("weights_loaded")
        weights2_loaded = sem("weights2_loaded")
        presets_done = sem("presets_done")
        eps_set = sem("eps_set")
        ident_ready = sem("ident_ready")
        dt_clipped = sem("dt_clipped")
        rates_ready = sem("rates_ready")
        logs_ready = sem("logs_ready")
        decay_terms = sem("decay_terms")
        decay_mean = sem("decay_mean")
        decay_row = sem("decay_row")
        decay_stored = sem("decay_stored")
        toep_loaded = sem("toep_loaded")
        flip_loaded = sem("flip_loaded")
        toep_flipped = sem("toep_flipped")
        toep_ready = sem("toep_ready")
        dt_sum = sem("dt_sum")
        dt_mean = sem("dt_mean")

        def value(pair, name, n):
            assert PRIME.get(name, 0) + n > 0, name
            return pair * total[name] + (PRIME.get(name, 0) + n)

        def wc_(name):
            a, b = W_AT[name]
            return W[:, a:b]

        def row(name):
            a, b = R_AT[name]
            return rows[:, a:b]

        def tab(name):
            a, b = T_AT[name]
            return rope[:, a:b]

        def parts(tile, d, which):
            first, step, n = which
            v = tile[:, :, MS:MS + 6 * d].rearrange("p h (s d) -> p h s d", d=d)
            return v[:, :, first:first + (n - 1) * step + 1:step, :]

        def value_view(tile, G, half, lo, hi):
            v = tile[:, half * 144:half * 144 + G * 256].rearrange("p (g c e) -> p g c e", c=8, e=32)
            return v[:, :, 0:4, lo:hi]

        def bf(m):
            return psM[:, m, :].bitcast(BF16)

        presets = [0]
        block = ctx.enter_context(nc.Block())

        @block.sync
        def _(sp):
            sp.dma_start(W[:, :], w_in).then_inc(weights_loaded, 16)
            sp.dma_start(rows[:, :], rows_in.partition_broadcast(128)).then_inc(weights_loaded, 16)
            sp.dma_start(rope[:, :], rope_in).then_inc(weights_loaded, 16)
            sp.dma_start(wc[:, :], wc_in).then_inc(weights_loaded, 16)
            sp.dma_start(y2[0][:, 0:128], flip_in).then_inc(flip_loaded, 16)
            sp.wait_ge(presets_done, 1)
            sp.dma_start(decay[:, 0:128], y1[0][0:NS, 0:128]).then_inc(decay_stored, 16)
            sp.wait_ge(decay_row, NS // 2)
            sp.dma_start(decay[:, 128:128 + S].unsqueeze(0), P[0:1, :, :, :].rearrange("p a b s -> p (a b) s")).then_inc(decay_stored, 16)
            sp.wait_ge(decay_stored, 32)
            sp.dma_start(toep[:, :, :], bass.AP(decay.tensor, 1, [[1, 128], [128 + S, NS], [1, S]])).then_inc(toep_loaded, 16)
            with sp.Fori(0, PAIRS) as pair:
                sp.wait_ge(a_drained, value(pair, "a_drained", 0))
                for j in range(2):
                    sp.dma_start(x[j][:, :, :], x_in[pair * 2 + j].rearrange("(t p) d -> p t d", p=128)).then_inc(x_loaded[j], 16)
                sp.dma_start(ctxk[:, :, :], ctx_in[:, pair, :, :]).then_inc(ctx_loaded, 16)
                for a in range(2):
                    sp.dma_start(ctxp[:, :, a, :], ctx_in[:, pair, :, :]).then_inc(ctx_loaded, 16)
                for s in steps:
                    L = LAYERS.get(s.L)
                    if s.kind in ("P3", "N") and not L["cross"]:
                        HB, wd = L["HB"], L["W"]
                        halves = H // HB // 4
                        view = qblk[s.L][s.j][:, :, :].rearrange("p (g a) s -> p g a s", a=HB)
                        for n in range(halves):
                            m, c = s.misc[f"q{n}"]
                            sp.wait_ge(misc_drained[m], value(pair, f"misc_drained{m}", c))
                            for a in range(HB):
                                lo = wd * a
                                if s.kind == "P3":
                                    sp.dma_start(view[lo:lo + wd, 4 * n:4 * n + 4, a, :],
                                                 QT[s.j][lo:lo + wd, 4 * n:4 * n + 4, :]).then_inc(qblk_loaded[s.j], 16)
                                else:
                                    sp.dma_start(view[lo:lo + MS, 4 * n:4 * n + 4, a, :],
                                                 QM[s.j][lo:lo + MS, 4 * n:4 * n + 4, :]).then_inc(mrow_loaded[s.j], 16)
                    if s.kind == "H" and s.L == "f":
                        sp.wait_ge(a_drained, value(pair, "a_drained", s.a + 1))
                        sp.dma_start(out[pair * 2 + s.j].rearrange("(t p) d -> p t d", p=128), yout[s.j][:, :, :]).then_inc(stored, 16)
            sp.wait_ge(stored, total["stored"] * PAIRS + PRIME["stored"])

        @block.gpsimd
        def _(pool):
            pool.memset(minus_half[:, :], -0.5).then_inc(eps_set, 1)
            pool.memset(ln_eps[:, :], LN_EPS).then_inc(eps_set, 1)
            pool.memset(rms_eps[:, :], RMS_EPS).then_inc(eps_set, 1)
            pool.memset(zero[:, :], 0.0).then_inc(eps_set, 1)
            pool.wait_ge(eps_set, 4)
            def preset(ap, v):
                presets[0] += 1
                pool.memset(ap, v).then_inc(presets_done, 1)

            preset(y1[0][:, :], 0.0)
            for j in range(2):
                for t in (qs[32][j], qs[64][j], ks["s0"][j], ks["s1"][j], qblk["s0"][j], qblk["s1"][j],
                          kblk["x0"][j], kblk["x1"][j], vx["x0"][j], vx["x1"][j], on4[j], gate[j]):
                    preset(t[:, :, :], 0.0)
                for t in (vp["s0"][j], vp["s1"][j]):
                    preset(t[:, :], 0.0)
            for t in (bdiag[0], kx["x0"], kx["x1"]):
                preset(t[:, :, :], 0.0)
            pool.wait_ge(presets_done, presets[0])
            for j in range(2):
                for t in (ks["s0"][j], ks["s1"][j]):
                    preset(t[:, :, 0:MS], 1.0)
                for half in range(2):
                    preset(value_view(vp["s0"][j], 4, half, DEN, DEN + 1), 1.0)
                    preset(value_view(vp["s1"][j], 2, half, DEN, DEN + 1), 1.0)
            for t in (kx["x0"], kx["x1"]):
                preset(t[:, :, 0:MS], 1.0)
            for half in range(2):
                pool.wait_ge(presets_done, presets[0])
                for j in range(2):
                    for name in ("x0", "x1"):
                        lo = 16 * half + DEN
                        preset(vx[name][j][64 * half:64 * half + 64, :, lo:lo + 1], 1.0)
            pool.wait_ge(presets_done, presets[0])
            for n, s in enumerate((a_drained, b_drained, p_used, a_filled, misc_drained[0], misc_drained[1],
                                   ot_drained[0], ot_drained[1], stored)):
                pool.memset(tokens[:, n:n + 1], 0.0).then_inc(s, tuple(PRIME.values())[n])

            with pool.Fori(0, PAIRS) as pair:
                done = [0]

                def mark(ins):
                    done[0] += 1
                    ins.then_inc(pool_step, 1)

                def settle():
                    pool.wait_ge(pool_step, value(pair, "pool_step", done[0]))

                def split(src, tile, d, which, rest, blank=None):
                    n = src.shape[1]
                    p1, p2, p3 = (parts(tile, d, w) for w in which)
                    a = src.unsqueeze(2)
                    nought = zero[:, :].unsqueeze(2).unsqueeze(3).broadcast_to([128, n, 3, d])
                    mark(pool.tensor_tensor(p1, a.broadcast_to([128, n, 3, d]), nought, ALU.subtract))
                    if blank is not None:
                        mark(pool.memset(blank, 0.0))
                    settle()
                    mark(pool.tensor_tensor(rest, src, p1[:, :, 0, :], ALU.subtract))
                    mark(pool.tensor_tensor(p2, a.broadcast_to([128, n, 2, d]), p1[:, :, 0:2, :], ALU.subtract))
                    settle()
                    return pool.tensor_tensor(p3[:, :, 0, :], rest, p2[:, :, 0, :], ALU.subtract)

                def rsqrt(s, j, k, src, eps):
                    n = s.after["stats_ready"] - marks(s)["stats_ready"] + k
                    pool.wait_ge(stats_ready, value(pair, "stats_ready", n))
                    mark(pool.tensor_tensor(veps[j][:, :], src, eps[:, :], ALU.add))
                    settle()
                    pool.tensor_tensor(rstd[j][:, :], veps[j][:, :], minus_half[:, :], ALU.pow).then_inc(rstd_ready, 1)

                for s in steps:
                    j = s.j
                    d = LAYERS[s.L]["d"] if s.L in LAYERS else 0
                    if s.kind in ("T1", "P1"):
                        rsqrt(s, j, 1, mv[j][:, :, 1], ln_eps)
                        if s.kind == "T1":
                            rsqrt(s, j, 2, mv[j][:, :, 1], ln_eps)
                        if s.L == "s1":
                            rsqrt(s, j, 2, ms[j][:, :], rms_eps)
                    if s.kind == "C":
                        if s.L == "x0":
                            m, c = s.misc["kv"]
                            pool.wait_ge(misc_drained[m], value(pair, f"misc_drained{m}", c))
                            n = 16
                        else:
                            pool.wait_ge(qk_ready, value(pair, "qk_ready", s.after["qk_ready"]))
                            n = 8
                        v = lambda t: t[:, 0:8 * n].rearrange("p (h d) -> p h d", d=8)
                        split(v(ckf), kx[s.L], d, K_PARTS, v(cres)).then_inc(split_done, 1)
                    if s.kind == "P3":
                        p2 = next(y for y in steps if (y.kind, y.L, y.j) == ("P2", s.L, j))
                        if s.L in ("x1",):
                            pool.wait_ge(qk_ready, value(pair, "qk_ready", p2.after["qk_ready"]))
                        else:
                            m, c = p2.misc["m"]
                            pool.wait_ge(misc_drained[m], value(pair, f"misc_drained{m}", c))
                        wd = LAYERS[s.L]["W"]
                        nq = T * H * d
                        v = lambda t: t.rearrange("p (h d) -> p h d", d=d)
                        if s.L in ks:
                            nk = T * (H if s.L == "s0" else 4) * d
                            mark(split(v(kf[j][:, :, :].rearrange("p t c -> p (t c)")[:, 0:nk]), ks[s.L][j], d, K_PARTS,
                                       v(qres[j][:, 0:nk])))
                        split(v(qf[j][:, :, :].rearrange("p t c -> p (t c)")[:, 0:nq]), qs[wd][j], d, Q_PARTS,
                              v(qres[j][:, 0:nq]), blank=qs[wd][j][:, :, 0:MS]).then_inc(split_done, 1)
                    if s.kind == "T6":
                        mark(pool.tensor_tensor(base[j][:, :, :], x[j][:, :, :], xn[j][:, :, :], ALU.add))
                        settle()
                        pool.tensor_tensor(base[j][:, :, :], base[j][:, :, :],
                                           row("bout").unsqueeze(1).broadcast_to([128, T, D]), ALU.add).then_inc(base_ready, 1)
                    if s.kind == "F3" and s.L != "s0":
                        if s.L == "s1":
                            f1 = next(y for y in steps if (y.kind, y.L, y.j) == ("F1", s.L, j))
                            m, c = f1.misc["m"]
                            pool.wait_ge(misc_drained[m], value(pair, f"misc_drained{m}", c))
                            other = on[j][:, :, :]
                        else:
                            other = row(s.L + "bo").unsqueeze(1).broadcast_to([128, T, D])
                        pool.tensor_tensor(base[j][:, :, :], x[j][:, :, :], other, ALU.add).then_inc(base_ready, 1)
                    if s.kind == "R2":
                        pool.tensor_tensor(base[j][:, :, :], x[j][:, :, :], xn[j][:, :, :], ALU.add).then_inc(base_ready, 1)
                    if s.kind == "H" and s.L == "f":
                        pool.tensor_tensor(base[j][:, :, :], x[j][:, :, :],
                                           row("fb2").unsqueeze(1).broadcast_to([128, T, D]), ALU.add).then_inc(base_ready, 1)
                assert done[0] == POOL_STEPS, done[0]

        @block.scalar
        def _(act):
            act.dma_start(w1[:, :], w1_in).then_inc(weights2_loaded, 16)
            act.dma_start(w2[:, :], w2_in).then_inc(weights2_loaded, 16)
            act.dma_start(b2[:, :], b2_in).then_inc(weights2_loaded, 16)
            act.dma_start(fw1[:, :], fw1_in).then_inc(weights2_loaded, 16)
            act.dma_start(fw2[:, :], fw2_in).then_inc(weights2_loaded, 16)
            act.wait_ge(weights_loaded, 64)
            act.activation(dt[:, 0:1], wc_("logdt"), ACT.Exp).then_inc(decay_terms, 1)
            act.activation(xm[0][:, 0:NS], wc_("alog"), ACT.Exp).then_inc(decay_terms, 1)
            act.wait_ge(logs_ready, 1)
            for s_ in range(NS):
                act.activation(toep[:, s_, :], row("iota"), ACT.Exp, scale=xm[1][:, s_:s_ + 1]).then_inc(decay_terms, 1)

            with act.Fori(0, PAIRS) as pair:
                def free(s, name):
                    m, c = s.misc[name]
                    act.wait_ge(misc_filled[m], value(pair, f"misc_filled{m}", c))
                    return m

                def claim(s, n):
                    name, count = p_release[s.b + n]
                    act.wait_ge(sems[name], value(pair, name, count))
                    act.wait_ge(b_filled, value(pair, "b_filled", s.b + n + 1))
                    return s.p[n]

                for s in steps:
                    j = s.j
                    if s.kind in ("T1", "P1"):
                        m = free(s, "m")
                        if s.kind == "T1":
                            act.activation(xnT[j][:, :], psM[:, m, 0:S], ACT.Identity, bias=wc_("lnb"), scale=wc_("lng")).then_inc(misc_drained[m], 1)
                        elif s.L == "s1":
                            act.activation(xnT[j][:, :], psM[:, m, 0:S], ACT.Identity, scale=wc_("rmsg")).then_inc(misc_drained[m], 1)
                        else:
                            act.copy(xnT[j][:, :], psM[:, m, 0:S]).then_inc(misc_drained[m], 1)
                    if s.kind == "T2":
                        m = free(s, "m")
                        act.activation(xpT[j][:, :], psM[:, m, 0:S], ACT.Identity, bias=wc_("bx"))
                        act.activation(zs[j][:, :], psM[:, m, S:2 * S], ACT.Silu, bias=wc_("bz")).then_inc(misc_drained[m], 1)
                    if s.kind == "T4":
                        m = free(s, "m")
                        act.copy(xm[j][:, :], psM[:, m, 0:S]).then_inc(misc_drained[m], 1)
                    if s.kind == "P3" and not LAYERS[s.L]["cross"]:
                        m = free(s, "k")
                        KG = LAYERS[s.L]["KG"]
                        act.copy(KT[j][:, 0:KG, :], bf(m)[:, 0:KG * S]).then_inc(misc_drained[m], 1)
                    if s.kind == "S":
                        for n in range(units(s)[1]):
                            p = claim(s, n)
                            act.activation(P[:, p, :, :].rearrange("p a s -> p (a s)"), psB[:, (s.b + n) % B_BANKS, :], ACT.Exp,
                                           scale=LAYERS[s.L]["scale"]).then_inc(b_drained, 1)
                    if s.kind == "G":
                        p = claim(s, 0)
                        bias = wc_("b1") if s.L == "s0" else wc_("fb1")
                        for f in range(2):
                            n = 2 * s.q + f
                            ins = act.activation(P[:, p, f, :], psB[:, s.b % B_BANKS, f * S:f * S + S], ACT.Gelu, bias=bias[:, n:n + 1])
                        ins.then_inc(b_drained, 1)
                    if s.kind == "F1":
                        v = next(y for y in steps if (y.kind, y.L, y.j, y.q) == ("V", s.L, j, 3 if LAYERS[s.L]["cross"] else 7))
                        act.wait_ge(p_used, value(pair, "p_used", v.after["p_used"]))
                        act.copy(ots[j][:, :, :].rearrange("p u s -> p (u s)"), psO[:, j, :, :].rearrange("p u s -> p (u s)")).then_inc(ot_drained[j], 1)
                    if s.kind == "F2":
                        m = free(s, "m")
                        act.copy(onT[j][:, :], psM[:, m, 0:S]).then_inc(misc_drained[m], 1)
                    if s.kind == "F3" and s.L == "s0":
                        m = free(s, "m")
                        act.activation(mlaT[j][:, :], psM[:, m, 0:S], ACT.Identity, bias=wc_("mlab")).then_inc(misc_drained[m], 1)
                    if s.kind == "R1":
                        act.wait_ge(logits_ready, value(pair, "logits_ready", s.after["logits_ready"]))
                        act.activation(lexp[j][:, :, :], lg[j][:, :, :], ACT.Exp).then_inc(router_exp, 1)
                    if s.kind == "R2":
                        m = free(s, "cT")
                        act.copy(gateT[j][:, :], psM[:, m, 0:S]).then_inc(misc_drained[m], 1)

        @block.vector
        def _(dve):
            dve.wait_ge(weights_loaded, 64)
            dve.tensor_copy(identb[:, :], wc_("ident")).then_inc(ident_ready, 1)
            dve.wait_ge(decay_terms, 2)
            dve.tensor_scalar(dt[:, 1:2], dt[:, 0:1], 1e-4, 1.0, ALU.max, ALU.min).then_inc(dt_clipped, 1)
            dve.wait_ge(dt_clipped, 1)
            dve.tensor_scalar(xm[1][:, 0:NS], xm[0][:, 0:NS], dt[:, 1:2], -1.0, ALU.mult, ALU.mult).then_inc(rates_ready, 1)
            dve.wait_ge(rates_ready, 1)
            dve.tensor_scalar(xm[1][:, 0:NS], xm[1][:, 0:NS], float(np.log(1e-8)), float(np.log1p(-1e-8)), ALU.max, ALU.min).then_inc(logs_ready, 1)
            dve.wait_ge(dt_sum, 1)
            dve.tensor_copy(dt[:, 2:3], psM[:, 0, 0:1]).then_inc(dt_mean, 1)
            for n in range(NS // 2):
                dve.wait_ge(decay_mean, n + 1)
                dve.tensor_copy(P[0:1, n, :, :].rearrange("p a s -> p (a s)"), psB[0:1, n % 2, :]).then_inc(decay_row, 1)
            for n in range(NS // 2):
                dve.wait_ge(toep_flipped, n + 1)
                dve.tensor_copy(toep[:, 2 * n:2 * n + 2, :].rearrange("p a s -> p (a s)"), psB[:, n % 2, :]).then_inc(toep_ready, 1)
            dve.wait_ge(presets_done, presets[0])

            with dve.Fori(0, PAIRS) as pair:
                done = [0]

                def mark(ins):
                    done[0] += 1
                    ins.then_inc(dve_step, 1)

                def settle():
                    dve.wait_ge(dve_step, value(pair, "dve_step", done[0]))

                def filled(s, name="m"):
                    m, c = s.misc[name]
                    dve.wait_ge(misc_filled[m], value(pair, f"misc_filled{m}", c))
                    return m

                def drained(s, name="m"):
                    m, c = s.misc[name]
                    dve.wait_ge(misc_drained[m], value(pair, f"misc_drained{m}", c))

                def moments(s, src, j, rms=False):
                    for t in range(T):
                        mark(dve.bn_stats(stats[j][:, t, :], src[:, t, :]))
                    settle()
                    dve.memset(wait_carrier[:, :], 0.0)
                    for t in range(T):
                        ins = dve.bn_aggr(mv[j][:, t, :], stats[j][:, t, :])
                        if rms or t == 0:
                            mark(ins)
                    if not rms:
                        ins.then_inc(stats_ready, 1)
                        return
                    settle()
                    mark(dve.tensor_tensor(ms[j][:, :], mv[j][:, :, 0], mv[j][:, :, 0], ALU.mult))
                    settle()
                    dve.tensor_tensor(ms[j][:, :], ms[j][:, :], mv[j][:, :, 1], ALU.add).then_inc(stats_ready, 1)

                def normalise(s, k, src, dst, j, final, rms=False):
                    n = s.after["rstd_ready"] - marks(s)["rstd_ready"] + k
                    dve.wait_ge(rstd_ready, value(pair, "rstd_ready", n))
                    for t in range(T):
                        if rms:
                            ins = dve.tensor_scalar(dst[:, t, :], src[:, t, :], rstd[j][:, t:t + 1], None, ALU.mult)
                        else:
                            ins = dve.tensor_scalar(dst[:, t, :], src[:, t, :], mv[j][:, t, 0:1], rstd[j][:, t:t + 1],
                                                    ALU.subtract, ALU.mult)
                        if not (final and t == T - 1):
                            mark(ins)
                    if final:
                        ins.then_inc(xn_ready, 1)

                prev = {0: None, 1: None}
                for s in steps:
                    j = s.j
                    L = LAYERS.get(s.L)
                    d = L["d"] if L else 0
                    if s.kind in ("T1", "P1"):
                        if s.kind == "T1":
                            dve.wait_ge(x_loaded[j], value(pair, f"x_loaded{j}", 16))
                        elif prev[j].kind == "H":
                            dve.wait_ge(a_drained, value(pair, "a_drained", prev[j].a + 1))
                        else:
                            drained(prev[j], "cb" if prev[j].kind == "R2" else "m")
                        moments(s, x[j], j)
                        twice = s.kind == "T1" or s.L == "s1"
                        normalise(s, 1, x[j], xn[j], j, not twice)
                        if twice:
                            settle()
                            moments(s, xn[j], j, rms=s.L == "s1")
                            normalise(s, 2, xn[j], xn2[j], j, True, rms=s.L == "s1")
                    if s.kind == "T3":
                        m = filled(s)
                        if j == 0:
                            dve.wait_ge(dt_mean, 1)
                        dve.tensor_scalar(bdiag[j][:, :, 0:NS * 33:33], psM[:, m, 0:T * NS].rearrange("p (t s) -> p t s", t=T),
                                          dt[:, 2:3], None, ALU.mult).then_inc(misc_drained[m], 1)
                    if s.kind == "T5":
                        m = filled(s)
                        dve.scalar_tensor_tensor(y1[j][:, :], xpT[j][:, :], wc_("dskip"), psM[:, m, 0:S],
                                                 ALU.mult, ALU.add).then_inc(misc_drained[m], 1)
                        drained(s)
                        dve.tensor_tensor(y2[j][:, :], y1[j][:, :], zs[j][:, :], ALU.mult).then_inc(y_ready, 1)
                    if s.kind == "T6" or (s.kind == "F3" and s.L != "s0"):
                        m = filled(s)
                        dve.wait_ge(base_ready, value(pair, "base_ready", s.after["base_ready"]))
                        dve.tensor_tensor(x[j][:, :, :].rearrange("p t d -> p (t d)"), psM[:, m, 0:S],
                                          base[j][:, :, :].rearrange("p t d -> p (t d)"), ALU.add).then_inc(misc_drained[m], 1)
                        prev[j] = s
                    if s.kind == "C":
                        m = filled(s, "kv")
                        ps = psM[:, m, :]
                        nk = 128 if s.L == "x0" else 32
                        for jj in range(2):
                            for a in range(2):
                                r = slice(64 * a, 64 * a + 64)
                                lo = nk + jj * nk
                                o = vx[s.L][jj][r, :, 16 * a:16 * a + 8]
                                if s.L == "x0":
                                    sel = lambda v: v.rearrange("p (h a d) -> p h a d", a=2, d=8)[:, :, a, :]
                                    mark(dve.tensor_tensor(o, sel(ps[r, lo:lo + nk]), sel(row("x0bv")[r, :]), ALU.add))
                                else:
                                    sel = lambda v: v.rearrange("p (g d) -> p g d", d=8).unsqueeze(2).broadcast_to([64, 4, 2, 8])
                                    mark(dve.tensor_tensor(o.rearrange("p (g r) d -> p g r d", r=2), sel(ps[r, lo:lo + nk]),
                                                           sel(row("x1bv")[r, :]), ALU.add))
                        if s.L == "x0":
                            dve.tensor_tensor(ckf[:, :], ps[:, 0:nk], row("x0bk"), ALU.add).then_inc(misc_drained[m], 1)
                        else:
                            dve.tensor_tensor(ck1[:, :], ps[:, 0:nk], row("x1bk"), ALU.add).then_inc(misc_drained[m], 1)
                            drained(s, "kv")
                            k3 = lambda t: t[:, :].rearrange("p (h d) -> p h d", d=8)
                            cs = lambda n, lo, hi: tab(n)[:, lo:hi].unsqueeze(1).broadcast_to([128, 4, hi - lo])
                            mark(dve.tensor_tensor(k3(ck2), k3(ck1), cs("kcos", 0, 8), ALU.mult))
                            mark(dve.tensor_tensor(k3(ck3)[:, :, 0:4], k3(ck1)[:, :, 4:8], cs("ksin", 0, 4), ALU.mult))
                            mark(dve.tensor_tensor(k3(ck3)[:, :, 4:8], k3(ck1)[:, :, 0:4], cs("ksin", 4, 8), ALU.mult))
                            settle()
                            wide = lambda t: k3(t).unsqueeze(2).broadcast_to([128, 4, 2, 8])
                            dve.tensor_tensor(ckf[:, 0:64].rearrange("p (g r d) -> p g r d", r=2, d=8), wide(ck2), wide(ck3),
                                              ALU.add).then_inc(qk_ready, 1)
                        m = filled(s, "kT")
                        n = L["KG"]
                        for jj in range(2):
                            for a in range(2):
                                r = slice(64 * a, 64 * a + 64)
                                ins = dve.tensor_copy(kblk[s.L][jj][r, :, 64 * a:64 * a + 64],
                                                      bf(m)[r, 0:n * 128].rearrange("p (g c) -> p g c", c=128)[:, :, 64 * jj:64 * jj + 64])
                                if (jj, a) != (1, 1):
                                    mark(ins)
                        ins.then_inc(misc_drained[m], 1)
                    if s.kind == "P2":
                        m = filled(s)
                        ps = psM[:, m, :]
                        flat = lambda t: t[:, :, :].rearrange("p t c -> p (t c)")
                        if s.L == "x0":
                            dve.tensor_tensor(flat(qf[j]), ps[:, 0:256], row("x0bq"), ALU.add).then_inc(misc_drained[m], 1)
                        elif s.L == "x1":
                            dve.tensor_tensor(flat(qt1[j]), ps[:, 0:256], row("x1bq"), ALU.add).then_inc(misc_drained[m], 1)
                            drained(s)
                            q4 = lambda t: t[:, :, :].rearrange("p t (h d) -> p t h d", d=8)
                            cs = lambda n, lo, hi: tab(n).rearrange("p (t d) -> p t d", d=8)[:, :, lo:hi].unsqueeze(2).broadcast_to([128, T, H, hi - lo])
                            mark(dve.tensor_tensor(q4(qt2[j])[:, :, :, 0:4], q4(qt1[j])[:, :, :, 4:8], cs("qsin", 0, 4), ALU.mult))
                            mark(dve.tensor_tensor(q4(qt2[j])[:, :, :, 4:8], q4(qt1[j])[:, :, :, 0:4], cs("qsin", 4, 8), ALU.mult))
                            mark(dve.tensor_tensor(q4(qf[j]), q4(qt1[j]), cs("qcos", 0, 8), ALU.mult))
                            settle()
                            dve.tensor_tensor(flat(qf[j]), flat(qf[j]), flat(qt2[j]), ALU.add).then_inc(qk_ready, 1)
                        elif s.L == "s0":
                            q = ps[:, 0:256].rearrange("p (t c) -> p t c", t=T)
                            fl = lambda t, n: flat(t)[:, 0:n].rearrange("p (t c) -> p t c", t=T)
                            mark(dve.tensor_tensor(fl(qf[j], 128), q[:, :, 0:64], row("s0bq").rearrange("p (t c) -> p t c", t=T), ALU.add))
                            mark(dve.tensor_tensor(fl(kf[j], 128), q[:, :, 64:128], row("s0bk").rearrange("p (t c) -> p t c", t=T), ALU.add))
                            for h in range(2):
                                vv = lambda v: v.rearrange("p (g h c d) -> p g h c d", h=2, c=4, d=4)[:, :, h, :, :]
                                o = value_view(vp["s0"][j], 4, h, 0, 4)
                                ins = dve.tensor_tensor(o, vv(ps[:, 256:384]), vv(row("s0bv")), ALU.add)
                                if h == 0:
                                    mark(ins)
                            ins.then_inc(misc_drained[m], 1)
                        else:
                            q = ps[:, 0:320].rearrange("p (t h d) -> p t h d", t=T, d=8)
                            rf = tab("rf").rearrange("p (t d) -> p t d", d=8).unsqueeze(2)
                            mark(dve.tensor_tensor(qf[j][:, :, :].rearrange("p t (h d) -> p t h d", d=8), q[:, :, 0:16, :],
                                                   rf.broadcast_to([128, T, 16, 8]), ALU.mult))
                            mark(dve.tensor_tensor(flat(kf[j])[:, 0:64].rearrange("p (t h d) -> p t h d", t=T, d=8), q[:, :, 16:20, :],
                                                   rf.broadcast_to([128, T, 4, 8]), ALU.mult))
                            for h in range(2):
                                o = value_view(vp["s1"][j], 2, h, 0, 8)
                                ins = dve.tensor_copy(o, ps[:, 320:384].rearrange("p (t c d) -> p t c d", t=T, d=8))
                                if h == 0:
                                    mark(ins)
                            ins.then_inc(misc_drained[m], 1)
                    if s.kind in ("P3", "N"):
                        if s.kind == "N":
                            q = qs[L["W"]][j]
                            nm = nmax[j][:, :, :].rearrange("p t h -> p (t h)")
                            last_a = [y for y in steps if (y.kind, y.L, y.j) == ("A", s.L, j)][-1]
                            dve.wait_ge(a_drained, value(pair, "a_drained", last_a.a + units(last_a)[0]))
                            mark(dve.tensor_copy(q[:, :, 0], nm))
                            settle()
                            dve.tensor_tensor(q[:, :, 1], nm, q[:, :, 0], ALU.subtract).then_inc(max_in_slots, 1)
                        dst = QT[j] if s.kind == "P3" else QM[j]
                        for n in range(max(H // L["HB"] // 4, 1)):
                            m = filled(s, f"q{n}")
                            dve.tensor_copy(dst[:, 4 * n:4 * n + 4, :].rearrange("p g s -> p (g s)"), bf(m)).then_inc(misc_drained[m], 1)
                    if s.kind == "A":
                        for n in range(units(s)[0]):
                            dve.wait_ge(a_filled, value(pair, "a_filled", s.a + n + 1))
                            ps = psA[:, (s.a + n) % A_BANKS, :]
                            if L["cross"]:
                                dve.tensor_reduce(nmax[j][:, :, 4 * s.q:4 * s.q + 4],
                                                  ps.rearrange("p (t h c) -> p t h c", t=T, c=C), AX.X, ALU.max,
                                                  negate=True).then_inc(a_drained, 1)
                            else:
                                h = 4 * s.q + n
                                dve.tensor_reduce(nmax[j][:, :, h], ps.rearrange("p (t c) -> p t c", t=T), AX.X, ALU.max,
                                                  negate=True).then_inc(a_drained, 1)
                    if s.kind == "F1":
                        m = filled(s)
                        ps = psM[:, m, :].rearrange("p (n e) -> p n e", e=16)
                        mark(dve.reciprocal(rden[j][:, :], ps[:, :, DEN]))
                        settle()
                        o = on4[j] if s.L == "s0" else on[j]
                        if L["cross"]:
                            dve.tensor_tensor(o[:, :, :].rearrange("p t (h d) -> p (t h) d", d=8), ps[:, :, 0:8],
                                              rden[j][:, :].unsqueeze(2).broadcast_to([128, 32, 8]), ALU.mult).then_inc(misc_drained[m], 1)
                        else:
                            for n in range(4):
                                t, u = n // 2, n % 2
                                oo = o[:, t, 8 * u * d:8 * u * d + 8 * d].rearrange("p (b c d) -> p c b d", b=2, d=d)
                                ii = ps[:, 8 * n:8 * n + 8, 0:d].rearrange("p (c b) d -> p c b d", b=2)
                                rr = rden[j][:, 8 * n:8 * n + 8].rearrange("p (c b) -> p c b", b=2).unsqueeze(3).broadcast_to([128, 4, 2, d])
                                ins = dve.tensor_tensor(oo, ii, rr, ALU.mult)
                                if n < 3:
                                    mark(ins)
                            ins.then_inc(misc_drained[m], 1)
                    if s.kind == "R1":
                        m = filled(s)
                        dve.tensor_tensor(lg[j][:, :, :].rearrange("p t e -> p (t e)"), psM[:, m, 0:T * E], row("rb"), ALU.add).then_inc(misc_drained[m], 1)
                        drained(s)
                        mark(dve.tensor_reduce(lmax[j][:, :], lg[j][:, :, :], AX.X, ALU.max))
                        settle()
                        bc = lambda v: v[:, :].unsqueeze(2).broadcast_to([128, T, E])
                        dve.tensor_tensor(lg[j][:, :, :], lg[j][:, :, :], bc(lmax[j]), ALU.subtract).then_inc(logits_ready, 1)
                        dve.wait_ge(router_exp, value(pair, "router_exp", s.after["router_exp"]))
                        mark(dve.tensor_reduce(gsum[j][:, :], lexp[j][:, :, :], AX.X, ALU.add))
                        settle()
                        mark(dve.reciprocal(gsum[j][:, :], gsum[j][:, :]))
                        settle()
                        p3 = prob[j][:, :].rearrange("p (t e) -> p t e", e=E)
                        mark(dve.tensor_tensor(p3, lexp[j][:, :, :], bc(gsum[j]), ALU.mult))
                        settle()
                        cube = lambda v: v[:, :].rearrange("p (n f) -> p n f", f=E)
                        c4 = lambda v: v[:, :].rearrange("p (t e f) -> p t e f", e=E, f=E)
                        others = p3.unsqueeze(2).broadcast_to([128, T, E, E])
                        mine4 = p3.unsqueeze(3).broadcast_to([128, T, E, E])
                        mark(dve.tensor_tensor(c4(above[j]), others, mine4, ALU.is_gt))
                        mark(dve.tensor_tensor(c4(ties[j]), others, mine4, ALU.is_equal))
                        settle()
                        mark(dve.tensor_tensor(ties[j][:, :], ties[j][:, :], row("tri"), ALU.mult))
                        settle()
                        mark(dve.tensor_tensor(above[j][:, :], above[j][:, :], ties[j][:, :], ALU.add))
                        settle()
                        mark(dve.tensor_reduce(rank[j][:, :], cube(above[j]), AX.X, ALU.add))
                        settle()
                        mark(dve.scalar_tensor_tensor(rank[j][:, :], rank[j][:, :], 2.0, prob[j][:, :], ALU.is_lt, ALU.mult))
                        settle()
                        r3 = rank[j][:, :].rearrange("p (t e) -> p t e", e=E)
                        mark(dve.tensor_reduce(gsum[j][:, :], r3, AX.X, ALU.add))
                        settle()
                        mark(dve.tensor_scalar(gsum[j][:, :], gsum[j][:, :], 1e-8, None, ALU.add))
                        settle()
                        mark(dve.reciprocal(gsum[j][:, :], gsum[j][:, :]))
                        settle()
                        mark(dve.tensor_scalar(gsum[j][:, :], gsum[j][:, :], 0.3, None, ALU.mult))
                        settle()
                        dve.tensor_tensor(gate[j][:, :, 0:E], r3, bc(gsum[j]), ALU.mult).then_inc(gates_ready, 1)
                    if s.kind == "R2":
                        m = filled(s, "cb")
                        dve.wait_ge(base_ready, value(pair, "base_ready", s.after["base_ready"]))
                        dve.tensor_tensor(x[j][:, :, :].rearrange("p t d -> p (t d)"), psM[:, m, 0:S],
                                          base[j][:, :, :].rearrange("p t d -> p (t d)"), ALU.add).then_inc(misc_drained[m], 1)
                        prev[j] = s
                    if s.kind == "H":
                        dve.wait_ge(a_filled, value(pair, "a_filled", s.a + 1))
                        ps = psA[:, s.a % A_BANKS, :]
                        if s.L == "s0":
                            if prev[j].kind == "R2":
                                drained(prev[j], "cb")
                            else:
                                dve.wait_ge(a_drained, value(pair, "a_drained", prev[j].a + 1))
                            for t in range(T):
                                ins = dve.scalar_tensor_tensor(x[j][:, t, :], ps[:, t * D:t * D + D], gate[j][:, t, s.q:s.q + 1],
                                                               x[j][:, t, :], ALU.mult, ALU.add)
                                if t == 0:
                                    mark(ins)
                            ins.then_inc(a_drained, 1)
                            prev[j] = s
                        else:
                            dve.wait_ge(base_ready, value(pair, "base_ready", s.after["base_ready"]))
                            dve.wait_ge(stored, value(pair, "stored", 0))
                            dve.tensor_tensor(yout[j][:, :, :].rearrange("p t d -> p (t d)"), ps[:, 0:S],
                                              base[j][:, :, :].rearrange("p t d -> p (t d)"), ALU.add).then_inc(a_drained, 1)
                assert done[0] == DVE_STEPS, done[0]

        @block.tensor
        def _(pe):
            pe.wait_ge(weights_loaded, 64)
            pe.wait_ge(ident_ready, 1)
            pe.wait_ge(dt_clipped, 1)
            pe.matmul(psM[:, 0, 0:1], wc_("ones"), dt[:, 1:2], start=True, stop=True).then_inc(dt_sum, 1)
            for n in range(NS // 2):
                pe.wait_ge(decay_terms, 2 + 2 * n + 2)
                if n >= 2:
                    pe.wait_ge(decay_row, n - 1)
                pe.matmul(psB[0:1, n % 2, :], wc_("ones")[:, 0:1], toep[:, 2 * n:2 * n + 2, :].rearrange("p a s -> p (a s)"),
                          start=True, stop=True).then_inc(decay_mean, 1)
            pe.wait_ge(decay_row, NS // 2)
            pe.wait_ge(dt_mean, 1)
            pe.wait_ge(flip_loaded, 16)
            pe.wait_ge(toep_loaded, 16)
            for n in range(NS // 2):
                if n >= 2:
                    pe.wait_ge(toep_ready, n - 1)
                pe.matmul(psB[:, n % 2, :], y2[0][:, 0:128], toep[:, 2 * n:2 * n + 2, :].rearrange("p a s -> p (a s)"),
                          start=True, stop=True).then_inc(toep_flipped, 1)
            pe.wait_ge(toep_ready, NS // 2)
            pe.wait_ge(presets_done, presets[0])
            pe.wait_ge(weights2_loaded, 80)

            with pe.Fori(0, PAIRS) as pair:
                def take(s, name="m"):
                    m, c = s.misc[name]
                    pe.wait_ge(misc_drained[m], value(pair, f"misc_drained{m}", c - 1))
                    return m

                def drained(s, name="m"):
                    m, c = s.misc[name]
                    pe.wait_ge(misc_drained[m], value(pair, f"misc_drained{m}", c))

                def reuse(name, unit, banks):
                    last = unit - banks
                    if last < 0:
                        last = max(k for k in range(total[name]) if k % banks == unit % banks) - total[name]
                    pe.wait_ge(sems[name], value(pair, name, last + 1))

                def to_columns(m, src):
                    for t in range(T):
                        ins = pe.transpose(psM[:, m, t * 128:t * 128 + 128], src[:, t, :], wc_("ident"))
                    return ins

                def find(kind, s, q=None):
                    return next(y for y in steps if (y.kind, y.L, y.j) == (kind, s.L, s.j) and (q is None or y.q == q))

                for s in steps:
                    j = s.j
                    L = LAYERS.get(s.L)
                    if s.kind in ("T1", "P1"):
                        m = take(s)
                        pe.wait_ge(xn_ready, value(pair, "xn_ready", s.after["xn_ready"]))
                        src = xn2[j] if s.kind == "T1" or s.L == "s1" else xn[j]
                        to_columns(m, src).then_inc(misc_filled[m], 1)
                    if s.kind == "T2":
                        drained(find("T1", s))
                        m = take(s)
                        for n in range(2):
                            ins = pe.matmul(psM[:, m, n * S:n * S + S], wc_("win")[:, n * D:n * D + D], xnT[j][:, :], start=True, stop=True)
                        ins.then_inc(misc_filled[m], 1)
                    if s.kind == "T3":
                        drained(find("T2", s))
                        m = take(s)
                        for t in range(T):
                            ins = pe.matmul(psM[:, m, t * NS:t * NS + NS], xpT[j][:, t * 128:t * 128 + 128], wc_("wb"), start=True, stop=True)
                        ins.then_inc(misc_filled[m], 1)
                    if s.kind == "T4":
                        drained(find("T3", s))
                        m = take(s)
                        for n in range(NS // 4):
                            for t in range(T):
                                for c in range(4):
                                    st = 4 * n + c
                                    ins = pe.matmul(psM[32 * c:32 * c + 32, m, t * 128:S], bdiag[j][:, t, st * 32:st * 32 + 32],
                                                    toep[:, st, 0:S - t * 128], start=(n == 0 and t == 0), stop=(n == 3 and t == 1),
                                                    skip_group_check=True)
                        ins.then_inc(misc_filled[m], 1)
                    if s.kind == "T5":
                        drained(find("T4", s))
                        m = take(s)
                        pe.matmul(psM[:, m, 0:S], wc[:, :], xm[j][:, :], start=True, stop=True).then_inc(misc_filled[m], 1)
                    if s.kind == "T6":
                        pe.wait_ge(y_ready, value(pair, "y_ready", s.after["y_ready"]))
                        m = take(s)
                        for t in range(T):
                            ins = pe.matmul(psM[:, m, t * D:t * D + D], y2[j][:, t * 128:t * 128 + 128], wc_("wout"), start=True, stop=True)
                        ins.then_inc(misc_filled[m], 1)
                    if s.kind == "C":
                        if s.L == "x0":
                            pe.wait_ge(ctx_loaded, value(pair, "ctx_loaded", 48))
                        m = take(s, "kv")
                        nk = 128 if s.L == "x0" else 32
                        pe.matmul(psM[:, m, 0:nk], ctxk[:, :, :], wc_(s.L + "k"), start=True, stop=True)
                        for jj in range(2):
                            lo = nk + jj * nk
                            ins = pe.matmul(psM[:, m, lo:lo + nk], ctxp[:, jj, :, :], wc_(s.L + "v"), start=True, stop=True)
                        ins.then_inc(misc_filled[m], 1)
                        m = take(s, "kT")
                        pe.wait_ge(split_done, value(pair, "split_done", s.after["split_done"]))
                        for g in range(L["KG"]):
                            ins = pe.transpose(bf(m)[:, g * 128:g * 128 + 128], kx[s.L][:, 2 * g:2 * g + 2, :], identb[:, :])
                        ins.then_inc(misc_filled[m], 1)
                    if s.kind == "P2":
                        drained(find("P1", s))
                        m = take(s)
                        lhs = [xnT[j][:, t * 128:t * 128 + 128] for t in range(T)]
                        if L["cross"]:
                            for t in range(T):
                                ins = pe.matmul(psM[:, m, t * D:t * D + D], lhs[t], wc_(s.L + "q"), start=True, stop=True)
                        else:
                            n = 128 if s.L == "s0" else 160
                            nv = 64 if s.L == "s0" else 32
                            for t in range(T):
                                pe.matmul(psM[:, m, t * n:t * n + n], lhs[t], wc_(s.L + "qk"), start=True, stop=True)
                            for t in range(T):
                                lo = T * n + t * nv
                                ins = pe.matmul(psM[:, m, lo:lo + nv], lhs[t], wc_(s.L + "v"), start=True, stop=True)
                        ins.then_inc(misc_filled[m], 1)
                    if s.kind in ("P3", "N"):
                        if s.kind == "P3":
                            pe.wait_ge(split_done, value(pair, "split_done", s.after["split_done"]))
                        else:
                            pe.wait_ge(max_in_slots, value(pair, "max_in_slots", s.after["max_in_slots"]))
                        HB, KG = L["HB"], L["KG"]
                        if s.kind == "P3" and not L["cross"]:
                            m = take(s, "k")
                            nh = T * H if s.L == "s0" else T * 4
                            for g in range(KG):
                                for t in range(T):
                                    h = t * nh // 2 + g * HB
                                    ins = pe.transpose(bf(m)[:, g * S + t * 128:g * S + t * 128 + 128],
                                                       ks[s.L][j][:, h:h + HB, :], identb[:, :])
                            ins.then_inc(misc_filled[m], 1)
                        for n in range(max(H // HB // 4, 1)):
                            m = take(s, f"q{n}")
                            for g in range(4):
                                for t in range(T):
                                    h = t * H + (4 * n + g) * HB
                                    ins = pe.transpose(bf(m)[:, g * S + t * 128:g * S + t * 128 + 128],
                                                       qs[L["W"]][j][:, h:h + HB, :], identb[:, :])
                            ins.then_inc(misc_filled[m], 1)
                    if s.kind == "A":
                        if s.q == 0:
                            p3 = find("P3", s)
                            if L["cross"]:
                                for n in range(2):
                                    drained(p3, f"q{n}")
                            else:
                                pe.wait_ge(qblk_loaded[j], value(pair, f"qblk_loaded{j}", p3.after[f"qblk_loaded{j}"]))
                                drained(p3, "k")
                        for n in range(units(s)[0]):
                            reuse("a_drained", s.a + n, A_BANKS)
                            ps = psA[:, (s.a + n) % A_BANKS, :]
                            if L["cross"]:
                                for t in range(T):
                                    for i in range(2):
                                        g = 2 * s.q + i
                                        lo = (2 * t + i) * 128
                                        ins = pe.matmul(ps[:, lo:lo + 128], QT[j][:, g, t * 128:t * 128 + 128],
                                                        kblk[s.L][j][:, g * L["KG"] // 8, :], start=True, stop=True)
                            else:
                                h = 4 * s.q + n
                                kg = (h // L["HB"]) % L["KG"]
                                for t in range(T):
                                    ins = pe.matmul(ps[:, t * S:t * S + S], qblk[s.L][j][:, h, t * 128:t * 128 + 128],
                                                    KT[j][:, kg, :], start=True, stop=True)
                            ins.then_inc(a_filled, 1)
                    if s.kind == "S":
                        if s.q == 0:
                            nn = find("N", s)
                            if L["cross"]:
                                for n in range(2):
                                    drained(nn, f"q{n}")
                            else:
                                pe.wait_ge(mrow_loaded[j], value(pair, f"mrow_loaded{j}", nn.after[f"mrow_loaded{j}"]))
                        for n in range(units(s)[1]):
                            reuse("b_drained", s.b + n, B_BANKS)
                            ps = psB[:, (s.b + n) % B_BANKS, :]
                            if L["cross"]:
                                for i in range(2):
                                    g = 2 * s.q + i
                                    ins = pe.matmul(ps[:, i * S:i * S + S], kblk[s.L][j][:, g * L["KG"] // 8, :], QM[j][:, g, :],
                                                    start=True, stop=True)
                            else:
                                h, kc = 4 * (s.q // 2) + 2 * n, s.q % 2
                                kg = (h // L["HB"]) % L["KG"]
                                ins = pe.matmul(ps, KT[j][:, kg, kc * 128:kc * 128 + 128],
                                                qblk[s.L][j][:, h:h + 2, :].rearrange("p a s -> p (a s)"), start=True, stop=True)
                            ins.then_inc(b_filled, 1)
                    if s.kind == "V":
                        sc = find("S", s, s.q)
                        nu = units(sc)[1]
                        pe.wait_ge(b_drained, value(pair, "b_drained", sc.b + nu))
                        if s.q == 0:
                            name = f"ot_drained{j}"
                            pe.wait_ge(ot_drained[j], value(pair, name, find("F1", s).after[name] - 1))
                        if L["cross"]:
                            for i in range(2):
                                g = 2 * s.q + i
                                c, u = g % 4, g // 4
                                ins = pe.matmul(psO[32 * c:32 * c + 32, j, u, :], vx[s.L][j][:, g, :], P[:, sc.p[0], i, :],
                                                start=True, stop=True, skip_group_check=True)
                        else:
                            four, kc = s.q // 2, s.q % 2
                            u, half = four // 2, four % 2
                            nh = 16 if s.L == "s0" else 8
                            for c in range(4):
                                lo = (kc * nh + (4 * four + c) % nh) * 32
                                ins = pe.matmul(psO[32 * c:32 * c + 32, j, u, :], vp[s.L][j][:, lo:lo + 32],
                                                P[:, sc.p[c // 2], c % 2, :],
                                                start=(half == 0 and kc == 0), stop=(half == 1 and kc == 1), skip_group_check=True)
                        ins.then_inc(p_used, nu)
                    if s.kind == "F1":
                        name = f"ot_drained{j}"
                        pe.wait_ge(ot_drained[j], value(pair, name, s.after[name]))
                        m = take(s)
                        for n in range(4):
                            t, u = n // 2, n % 2
                            ins = pe.transpose(psM[:, m, n * 128:n * 128 + 128], ots[j][:, u, t * 128:t * 128 + 128], wc_("ident"))
                        ins.then_inc(misc_filled[m], 1)
                    if s.kind == "F2":
                        drained(find("F1", s))
                        m = take(s)
                        to_columns(m, on4[j] if s.L == "s0" else on[j]).then_inc(misc_filled[m], 1)
                    if s.kind == "F3":
                        drained(find("F2", s))
                        m = take(s)
                        if s.L == "s0":
                            ins = pe.matmul(psM[:, m, 0:S], wc_("s0o"), onT[j][:, :], start=True, stop=True)
                        else:
                            for t in range(T):
                                ins = pe.matmul(psM[:, m, t * D:t * D + D], onT[j][:, t * 128:t * 128 + 128], wc_(s.L + "o"), start=True, stop=True)
                        ins.then_inc(misc_filled[m], 1)
                    if s.kind == "R1":
                        drained(find("F3", s))
                        m = take(s)
                        for t in range(T):
                            ins = pe.matmul(psM[:, m, t * E:t * E + E], mlaT[j][:, t * 128:t * 128 + 128], wc_("router"), start=True, stop=True)
                        ins.then_inc(misc_filled[m], 1)
                    if s.kind == "R2":
                        pe.wait_ge(gates_ready, value(pair, "gates_ready", s.after["gates_ready"]))
                        m = take(s, "cT")
                        to_columns(m, gate[j]).then_inc(misc_filled[m], 1)
                        drained(s, "cT")
                        m = take(s, "cb")
                        for t in range(T):
                            ins = pe.matmul(psM[:, m, t * D:t * D + D], gateT[j][:, t * 128:t * 128 + 128], b2[:, :], start=True, stop=True)
                        ins.then_inc(misc_filled[m], 1)
                    if s.kind == "G":
                        if s.L == "f" and s.q == 0:
                            drained(find("P1", s))
                        src, w = (mlaT[j], w1) if s.L == "s0" else (xnT[j], fw1)
                        reuse("b_drained", s.b, B_BANKS)
                        for f in range(2):
                            n = 2 * s.q + f
                            ins = pe.matmul(psB[:, s.b % B_BANKS, f * S:f * S + S], w[:, n * 128:n * 128 + 128], src[:, :], start=True, stop=True)
                        ins.then_inc(b_filled, 1)
                    if s.kind == "H":
                        gs = [find("G", s, s.q)] if s.L == "s0" else [find("G", s, 0), find("G", s, 1)]
                        w = w2 if s.L == "s0" else fw2
                        pe.wait_ge(b_drained, value(pair, "b_drained", gs[-1].b + 1))
                        reuse("a_drained", s.a, A_BANKS)
                        last = 2 * len(gs) - 1
                        for t in range(T):
                            for n in range(last + 1):
                                g = gs[n // 2]
                                k = 2 * s.q + n
                                ins = pe.matmul(psA[:, s.a % A_BANKS, t * D:t * D + D], P[:, g.p[0], n % 2, t * 128:t * 128 + 128],
                                                w[:, k * D:k * D + D], start=(n == 0), stop=(n == last))
                        ins.then_inc(a_filled, 1)


def kernel(**inputs):
    from concourse import bacc
    from concourse.bass_utils import run_bass_kernel_spmd

    g = {k: np.asarray(v) for k, v in inputs.items()}
    f32 = np.float32

    def pack(table, parts):
        assert [n for n, _ in table] == list(parts), [n for n, _ in table]
        out = [np.asarray(parts[n], f32).reshape(-1, w) for n, w in table]
        return np.ascontiguousarray(np.concatenate(out, axis=1))

    heads4 = lambda w: w.reshape(w.shape[0], H, 8)[:, :, :4].reshape(w.shape[0], 64)
    w = pack(W_COLS, {
        "win": g["L0_attn_W_in"].T, "wb": g["L0_attn_W_B"].T, "wout": g["L0_attn_W_out"].T,
        "x0q": g["L0_xattn_w_q"].T, "x0k": g["L0_xattn_w_k"].T, "x0v": g["L0_xattn_w_v"].T, "x0o": g["L0_xattn_w_o"].T,
        "x1q": g["L1_xattn_Wq"].T, "x1k": g["L1_xattn_Wk"].T, "x1v": g["L1_xattn_Wv"].T, "x1o": g["L1_xattn_Wo"].T,
        "s0qk": np.concatenate([heads4(g["L0_ffn_q_w"]), g["L0_ffn_k_w"]], axis=1), "s0v": g["L0_ffn_v_w"], "s0o": g["L0_ffn_o_w"],
        "router": g["L0_ffn_router_w"],
        "s1qk": np.concatenate([g["L1_attn_w_q"], g["L1_attn_w_k"]], axis=1), "s1v": g["L1_attn_w_v"], "s1o": g["L1_attn_w_o"],
        "ident": np.eye(128, dtype=f32), "ones": np.full((128, 128), 1.0 / D, f32),
        "bx": g["L0_attn_b_in"][:D], "bz": g["L0_attn_b_in"][D:], "dskip": g["L0_attn_D_skip"],
        "lng": g["L0_attn_ln_g"], "lnb": g["L0_attn_ln_b"], "rmsg": g["L1_attn_g"], "mlab": g["L0_ffn_o_b"],
        "logdt": g["L0_attn_log_dt"], "alog": g["L0_attn_A_log"],
        "b1": g["L0_ffn_b1"].reshape(16, 128).T, "fb1": g["L1_ffn_b1"].reshape(4, 128).T,
    })
    twice = lambda v: np.concatenate([v, v])
    rows = pack(R_COLS, {
        "bout": g["L0_attn_b_out"], "x0bq": twice(g["L0_xattn_b_q"]), "x0bk": g["L0_xattn_b_k"], "x0bv": g["L0_xattn_b_v"],
        "x0bo": g["L0_xattn_b_o"], "x1bq": twice(g["L1_xattn_bq"]), "x1bk": g["L1_xattn_bk"], "x1bv": g["L1_xattn_bv"],
        "x1bo": g["L1_xattn_bo"], "s0bq": twice(heads4(g["L0_ffn_q_b"][None])[0]), "s0bk": twice(g["L0_ffn_k_b"]),
        "s0bv": twice(g["L0_ffn_v_b"]), "rb": twice(g["L0_ffn_router_b"]), "fb2": g["L1_ffn_b2"],
        "tri": twice(np.tril(np.ones((E, E), f32), -1).reshape(-1)), "iota": np.arange(S, dtype=f32),
    })[0]
    pos, dims = np.arange(S, dtype=f32), np.arange(8)
    theta = np.power(f32(10000.0), (-2.0 * (dims // 2) / 8).astype(f32)).astype(f32)
    ang = (pos[:, None] * theta[None, :]).astype(f32)
    sign = np.where(np.arange(S) % 2 == 1, -1.0, 1.0).astype(f32)
    rf = np.cos(ang) + sign[:, None] * np.sin(ang)
    freq = (1.0 / f32(10000.0) ** (np.arange(0, 8, 2, dtype=f32) / f32(8))).astype(f32)
    emb = np.concatenate([np.outer(pos, freq)] * 2, axis=1).astype(f32)
    cos = np.cos(emb)
    sin = np.sin(emb) * np.where(dims < 4, -1.0, 1.0).astype(f32)
    tiles = lambda t: t.reshape(T, 128, 8).transpose(1, 0, 2).reshape(128, 16)
    rope = pack(T_COLS, {"rf": tiles(rf), "qcos": tiles(cos), "qsin": tiles(sin),
                         "kcos": np.concatenate([cos[:C]] * 2), "ksin": np.concatenate([sin[:C]] * 2)})
    wc = np.zeros((128, D), f32)
    for c in range(4):
        wc[32 * c:32 * c + NS] = g["L0_attn_W_C"].T
    b2 = np.zeros((128, D), f32)
    b2[:E] = g["L0_ffn_b2"]
    arrays = {
        "x": g["x"],
        "context": g["ctx_1024"].reshape(PAIRS, 2, C, D).transpose(3, 0, 1, 2),
        "weights": w,
        "expert_w1": g["L0_ffn_w1"].transpose(1, 0, 2).reshape(D, -1),
        "expert_w2": g["L0_ffn_w2"].reshape(E, 2, 128, D).transpose(2, 0, 1, 3).reshape(128, -1),
        "expert_b2": b2,
        "mlp_w1": g["L1_ffn_w1"],
        "mlp_w2": g["L1_ffn_w2"].reshape(4, 128, D).transpose(1, 0, 2).reshape(128, -1),
        "state_out": wc,
        "bias_rows": rows,
        "positions": rope,
        "flip": np.eye(128, dtype=f32)[::-1],
    }
    arrays = {k: np.ascontiguousarray(v) for k, v in arrays.items()}
    nc = bacc.Bacc("TRN2", target_bir_lowering=False, num_devices=1)
    aps = [nc.dram_tensor(n, a.shape, mybir.dt.from_np(a.dtype), kind="ExternalInput").ap() for n, a in arrays.items()]
    out = nc.dram_tensor("y", (B, S, D), F32, kind="ExternalOutput").ap()
    decoder(nc, *aps, out)
    result = run_bass_kernel_spmd(nc, [arrays], core_ids=[0])
    return result.results[0]["y"]
```

```python
from contextlib import ExitStack

import numpy as np

import concourse.bass as bass
import concourse.mybir as mybir

F32 = mybir.dt.float32
BF16 = mybir.dt.bfloat16
ALU = mybir.AluOpType
ACT = mybir.ActivationFunctionType
AX = mybir.AxisListType

B, S, D, C = 8, 256, 128, 64
T = S // 128
PAIRS = B // 2
H = 16
NS = 16
E = 8
MS = 2
DEN = 8
LN_EPS = 1e-5
RMS_EPS = float(np.finfo(np.float32).eps)

LAYERS = {
    "x0": dict(d=8, W=64, HB=2, KG=8, scale=8.0 ** -0.5, cross=True),
    "s0": dict(d=4, W=32, HB=4, KG=4, scale=0.5, cross=False),
    "s1": dict(d=8, W=64, HB=2, KG=2, scale=128.0 ** -0.5, cross=False),
    "x1": dict(d=8, W=64, HB=2, KG=4, scale=8.0 ** -0.5, cross=True),
}
Q_PARTS = ((0, 1, 3), (3, 2, 2), (4, 1, 1))
K_PARTS = ((2, 1, 3), (0, 5, 2), (1, 1, 1))

A_BANKS, B_BANKS, P_SLOTS = 2, 2, 4

W_COLS = [("ident", 128), ("ones", 128),
          ("bx", 1), ("bz", 1), ("dskip", 1), ("lng", 1), ("lnb", 1), ("rmsg", 1), ("mlab", 1),
          ("logdt", 1), ("alog", NS), ("b1", 16), ("fb1", 4),
          ("win", 256), ("wb", 16), ("wout", 128),
          ("x0q", 128), ("x0k", 128), ("x0v", 128), ("x0o", 128),
          ("x1q", 128), ("x1k", 32), ("x1v", 32), ("x1o", 128),
          ("s0qk", 128), ("s0v", 64), ("s0o", 128), ("router", 8),
          ("s1qk", 160), ("s1v", 32), ("s1o", 128)]
R_COLS = [("iota", 256), ("bout", 128), ("x0bq", 256), ("x0bk", 128), ("x0bv", 128), ("x0bo", 128),
          ("x1bq", 256), ("x1bk", 32), ("x1bv", 32), ("x1bo", 128),
          ("s0bq", 128), ("s0bk", 128), ("s0bv", 128), ("rb", 16), ("fb2", 128),
          ("tri", 128)]
T_COLS = [("rf", 16), ("qcos", 16), ("qsin", 16), ("kcos", 8), ("ksin", 8)]


def columns(table):
    at, out = 0, {}
    for name, width in table:
        out[name] = (at, at + width)
        at += width
    return out, at


W_AT, W_N = columns(W_COLS)
R_AT, R_N = columns(R_COLS)
T_AT, T_N = columns(T_COLS)


def find(steps, kind, s, q=None):
    return [y for y in steps if (y.kind, y.L, y.j) == (kind, s.L, s.j) and (q is None or y.q == q)][-1]


class Step:

    def __init__(self, kind, L=None, j=0, q=0):
        self.kind, self.L, self.j, self.q = kind, L, j, q


def norms(L):
    return 2 if L in ("m", "s1") else 1


def stream(j):
    out = [Step("T1", "m", j, q) for q in range(3)] + [Step(k, "m", j) for k in ("T2", "T3", "T4", "T5", "T6")]

    def attention(L):
        out.extend(Step("P1", L, j, q) for q in range(1 + norms(L)))
        out.extend([Step("P2", L, j), Step("P3", L, j, 0), Step("P3", L, j, 1)])
        order = ("A0 P2 A1 N0 N1 A2 S0 A3 S1 N2 V0 N3 V1 S2 S3 V2 V3" if LAYERS[L]["cross"] else
                 "A0 P2 A1 N0 N1 A2 S0 S1 V0 A3 S2 V1 N2 S3 V2 N3 S4 V3 S5 V4 S6 V5 S7 V6 V7")
        out.extend(Step("P3" if name == "P2" else name[0], L, j, int(name[1])) for name in order.split())
        out.extend([Step("F1", L, j), Step("F2", L, j), Step("F3", L, j)])

    attention("x0")
    attention("s0")
    out.extend([Step("R1", "s0", j, 0), Step("G", "s0", j, 0), Step("R1", "s0", j, 1)])
    out.extend([Step("R2", "s0", j), Step("R3", "s0", j)])
    for e in range(1, E):
        out.append(Step("G", "s0", j, e))
        out.append(Step("H", "s0", j, e - 1))
    out.append(Step("H", "s0", j, E - 1))
    attention("s1")
    attention("x1")
    out.extend([Step("P1", "f", j, 0), Step("P1", "f", j, 1), Step("G", "f", j, 0), Step("G", "f", j, 1), Step("H", "f", j, 0)])
    return out


ORDER = (
    "0101c01010c0100010100101000100110000001010c01010100101110101110c1110011100101001"
    "00001001000010001010010100110010111111011110101111110011101000100100001100000010"
    "11011011110100111101001001100010000010001010010011011000101011011111001111101101"
    "1110110101100100010100001010101001011011101111101101110110011101")


def schedule():
    todo = {"0": stream(0), "1": stream(1), "c": [Step("C", L, 0, q) for L in ("x0", "x1") for q in range(2)]}
    return [todo[n].pop(0) for n in ORDER if todo[n]]


def misc_names(s):
    L = LAYERS.get(s.L, {})
    if s.kind == "P3":
        return ([], (["m"] if L["cross"] else ["k", "m"]), ["m"])[s.q]
    if s.kind == "N":
        return ["m"] if s.q % 2 else []
    if s.kind in ("T1", "P1"):
        return ["m"] if s.q == norms(s.L) else []
    if s.kind == "R1":
        return ["m"] if s.q == 0 else []
    if s.kind in ("C", "T2", "T3", "T4", "T5", "T6", "P2", "F1", "F2", "F3", "R2", "R3"):
        return ["m"]
    return []


def drainers(s, name):
    return 2 if s.kind in ("P3", "N") and name != "k" and not LAYERS[s.L]["cross"] else 1


def units(s):
    cross = s.L in LAYERS and LAYERS[s.L]["cross"]
    if s.kind == "A":
        return (1 if cross else 4), 0
    if s.kind == "S":
        return 0, (1 if cross else 2)
    if s.kind == "G":
        return 0, 1
    if s.kind == "H":
        return 1, 0
    return 0, 0


def marks(s):
    out = {}
    cross = s.L in LAYERS and LAYERS[s.L]["cross"]
    if s.kind in ("T1", "P1"):
        out.update(dict(xn_ready=1) if s.q == norms(s.L) else dict(stats_ready=1, rstd_ready=1))
    if s.kind == "P2" and s.L == "x1":
        out["qk_ready"] = 1
    if s.kind == "C" and s.L == "x1" and s.q == 0:
        out["qk_ready"] = 1
    if s.kind == "C" and s.q == 0 or (s.kind == "P3" and s.q == 0 and not cross):
        out["k_split"] = 1
    if s.kind == "P3" and s.q == 0:
        out.update(q_part1=1, q_split=1)
    if s.kind == "N" and s.q % 2 == 0:
        out["max_in_slots"] = 1
    if s.kind == "T5":
        out["y_ready"] = 1
    if s.kind in ("T6", "F3", "R3") or (s.kind == "H" and s.L == "f"):
        if not (s.kind == "F3" and s.L == "s0"):
            out["base_ready"] = 1
    if s.kind == "F1":
        out[f"ot_drained{s.j}"] = 1
    if s.kind == "V":
        out["p_used"] = 1 if cross else 2
    if s.kind == "R1":
        out.update(dict(gates_ready=1) if s.q else dict(logits_ready=1, router_exp=1))
    if s.kind == "H" and s.L == "f":
        out[f"stored{s.j}"] = 16
    return out


def number(steps):
    k = a = b = 0
    total, fills, drains, slots = {}, [0, 0], [0, 0], [0, 0]
    for s in steps:
        s.misc = {}
        for name in misc_names(s):
            bank = k % 2
            before = drains[bank]
            fills[bank] += 1
            drains[bank] += drainers(s, name)
            s.misc[name] = (bank, fills[bank], before, drains[bank])
            k += 1
        na, nb = units(s)
        s.a, s.b = a, b
        a += na
        b += nb
        s.p = [s.j * P_SLOTS + (slots[s.j] + n) % P_SLOTS for n in range(nb)]
        slots[s.j] += nb
        for name, n in marks(s).items():
            total[name] = total.get(name, 0) + n
        s.after = dict(total)
    used = []
    for s in steps:
        if s.kind == "S":
            v = next(x for x in steps if (x.kind, x.L, x.j, x.q) == ("V", s.L, s.j, s.q))
            used += [(p, "p_used", v.after["p_used"]) for p in s.p]
        if s.kind == "G":
            h = next(x for x in steps if (x.kind, x.L, x.j, x.q) == ("H", s.L, s.j, s.q if s.L == "s0" else 0))
            used += [(p, "a_filled", h.a + 1) for p in s.p]
    assert len(used) == b
    total.update(a_filled=a, a_drained=a, b_filled=b, b_drained=b)
    for m in range(2):
        total[f"misc_filled{m}"], total[f"misc_drained{m}"] = fills[m], drains[m]
    release = {}
    for unit, (p, _, _) in enumerate(used):
        before = [u for u in range(unit) if used[u][0] == p]
        last = before[-1] if before else max(u for u in range(b) if used[u][0] == p)
        _, name, n = used[last]
        release[unit] = (name, n if before else n - total[name])
    return total, release


DVE_STEPS, POOL_STEPS = 223, 36


def decoder(nc, x_in, ctx_in, w_in, w1_in, w2_in, b2_in, fw1_in, fw2_in, wc_in, rows_in, rope_in, flip_in, out):
    steps = schedule()
    total, p_release = number(steps)
    total.update(dve_step=DVE_STEPS, pool_step=POOL_STEPS, x_loaded0=16, x_loaded1=16, ctx_loaded=48)
    PRIME = dict(a_drained=A_BANKS, b_drained=B_BANKS, p_used=total["p_used"], a_filled=total["a_filled"],
                 misc_drained0=1, misc_drained1=1, ot_drained0=1, ot_drained1=1, stored0=16, stored1=16)

    with ExitStack() as ctx:
        def sb(name, shape, dt=F32):
            return ctx.enter_context(nc.sbuf_tensor(name, shape, dt))

        def both(name, shape, dt=F32):
            return [sb(f"{name}{j}", shape, dt) for j in range(2)]

        def sem(name):
            return ctx.enter_context(nc.semaphore(name))

        W = sb("W", [128, W_N])
        w1 = sb("w1", [128, E * 2 * 128])
        w2 = sb("w2", [128, E * 2 * D])
        fw1 = sb("fw1", [128, 512])
        fw2 = sb("fw2", [128, 4 * D])
        b2 = sb("b2", [128, D])
        wc = sb("wc", [128, D])
        rows = sb("rows", [128, R_N])
        rope = sb("rope", [128, T_N])
        identb = sb("identb", [128, 128], BF16)
        minus_half = sb("minus_half", [128, T])
        zero = sb("zero", [128, 1])
        wait_carrier = sb("wait_carrier", [128, 1])
        ln_eps = sb("ln_eps", [128, T])
        rms_eps = sb("rms_eps", [128, T])
        dt = sb("dt", [128, 4])
        tokens = sb("tokens", [128, 10])
        toep = sb("toep", [128, NS, S])

        x = both("x", [128, T, D])
        base = both("base", [128, T, D])
        xn = both("xn", [128, T, D])
        xn2 = both("xn2", [128, T, D])
        xnT = both("xnT", [128, S])
        stats = both("stats", [128, T, 6])
        mv = both("mv", [128, T, 2])
        ms = both("ms", [128, T])
        veps = both("veps", [128, T])
        rstd = both("rstd", [128, T])
        xpT = both("xpT", [128, S])
        zs = both("zs", [128, S])
        bdiag = [sb("bdiag", [128, T, NS * 32 + 32])] * 2
        xm = both("xm", [128, S])
        y1 = both("y1", [128, S])
        y2 = both("y2", [128, S])
        qf = both("qf", [128, T, 128])
        qt1 = [y1[j][:, :].rearrange("p (t c) -> p t c", t=T) for j in range(2)]
        qt2 = [y2[j][:, :].rearrange("p (t c) -> p t c", t=T) for j in range(2)]
        kf = both("kf", [128, T, 64])
        qres = both("qres", [128, 256])
        kres = both("kres", [128, 128])
        qs = {32: both("qs32_", [128, T * H, 32], BF16), 64: both("qs64_", [128, T * H, 64], BF16)}
        ks = {"s0": both("ks_s0", [128, T * H, 32], BF16), "s1": both("ks_s1", [128, T * 4, 64], BF16)}
        QT = both("QT", [128, 8, S], BF16)
        KT = both("KT", [128, 4, S], BF16)
        qblk = {"s0": both("qblk_s0", [128, H, S], BF16), "s1": both("qblk_s1", [128, H, S], BF16)}
        vp = {"s0": both("vp_s0", [128, T * H * 32 + 160]), "s1": both("vp_s1", [128, T * 8 * 32 + 160])}
        nmax = both("nmax", [128, T, H])
        ots = both("ots", [128, 2, S])
        rden = both("rden", [128, 32])
        on = both("on", [128, T, D])
        on4 = both("on4", [128, T, D])
        zt = [on[j][:, :, :].rearrange("p t d -> p (t d)") for j in range(2)]
        onT = xpT
        mlaT = xm
        lg = both("lg", [128, T, E])
        lmax = both("lmax", [128, T])
        lexp = both("lexp", [128, T, E])
        gsum = both("gsum", [128, T])
        prob = both("prob", [128, T * E])
        above = [y1[j][:, 0:T * E * E] for j in range(2)]
        ties = [y1[j][:, T * E * E:2 * T * E * E] for j in range(2)]
        rank = both("rank", [128, T * E])
        gate = both("gate", [128, T, 128])
        gateT = zs
        yout = both("yout", [128, T, D])
        ctxk = sb("ctxk", [128, 2, C])
        ctxp = sb("ctxp", [128, 2, 2, C])
        ckf = sb("ckf", [128, 128])
        ck1 = sb("ck1", [128, 32])
        ck2 = sb("ck2", [128, 32])
        ck3 = sb("ck3", [128, 32])
        cres = sb("cres", [128, 128])
        kx = {"x0": sb("kx0", [128, 16, 64], BF16), "x1": sb("kx1", [128, 8, 64], BF16)}
        kblk = {"x0": both("kblk0", [128, 8, 128], BF16), "x1": both("kblk1", [128, 4, 128], BF16)}
        vx = {"x0": both("vx0", [128, 8, 32]), "x1": both("vx1", [128, 8, 32])}
        P = sb("P", [128, 2 * P_SLOTS, 2, S])

        psA = ctx.enter_context(nc.psum_tensor("psA", [128, A_BANKS, 512], F32))
        psB = ctx.enter_context(nc.psum_tensor("psB", [128, B_BANKS, 512], F32))
        psO = ctx.enter_context(nc.psum_tensor("psO", [128, 2, 2, S], F32))
        psM = ctx.enter_context(nc.psum_tensor("psM", [128, 2, 512], F32))
        decay = nc.dram_tensor("decay_rows", [NS, 128 + S], F32, kind="Internal").ap()

        names = ["a_filled", "a_drained", "b_filled", "b_drained", "p_used",
                 "stats_ready", "rstd_ready", "xn_ready", "qk_ready", "k_split", "q_split",
                 "q_part1", "max_in_slots", "y_ready", "base_ready",
                 "logits_ready", "router_exp", "gates_ready", "ctx_loaded", "dve_step", "pool_step"]
        sems = {n: sem(n) for n in names}
        (a_filled, a_drained, b_filled, b_drained, p_used, stats_ready, rstd_ready, xn_ready, qk_ready,
         k_split, q_split, q_part1, max_in_slots, y_ready, base_ready,
         logits_ready, router_exp, gates_ready, ctx_loaded,
         dve_step, pool_step) = (sems[n] for n in names)
        misc_filled = [sem(f"misc_filled{m}") for m in range(2)]
        misc_drained = [sem(f"misc_drained{m}") for m in range(2)]
        stored = [sem(f"stored{j}") for j in range(2)]
        x_loaded = [sem(f"x_loaded{j}") for j in range(2)]
        ot_drained = [sem(f"ot_drained{j}") for j in range(2)]
        weights_loaded = sem("weights_loaded")
        weights2_loaded = sem("weights2_loaded")
        presets_done = sem("presets_done")
        eps_set = sem("eps_set")
        ident_ready = sem("ident_ready")
        dt_clipped = sem("dt_clipped")
        rates_ready = sem("rates_ready")
        logs_ready = sem("logs_ready")
        decay_terms = sem("decay_terms")
        decay_mean = sem("decay_mean")
        decay_row = sem("decay_row")
        decay_stored = sem("decay_stored")
        toep_loaded = [sem(f"toep_loaded{n}") for n in range(4)]
        early_loaded = sem("early_loaded")
        blocks_blank = sem("blocks_blank")
        flip_loaded = sem("flip_loaded")
        toep_flipped = sem("toep_flipped")
        toep_ready = sem("toep_ready")
        dt_sum = sem("dt_sum")
        half_bias_ready = sem("half_bias_ready")
        dt_mean = sem("dt_mean")

        def value(pair, name, n):
            assert PRIME.get(name, 0) + n > 0, name
            return pair * total[name] + (PRIME.get(name, 0) + n)

        def wc_(name):
            a, b = W_AT[name]
            return W[:, a:b]

        def row(name):
            a, b = R_AT[name]
            return rows[:, a:b]

        def tab(name):
            a, b = T_AT[name]
            return rope[:, a:b]

        def parts(tile, d, which):
            first, step, n = which
            v = tile[:, :, MS:MS + 6 * d].rearrange("p h (s d) -> p h s d", d=d)
            return v[:, :, first:first + (n - 1) * step + 1:step, :]

        def value_view(tile, G, half, lo, hi):
            v = tile[:, half * 144:half * 144 + G * 256].rearrange("p (g c e) -> p g c e", c=8, e=32)
            return v[:, :, 0:4, lo:hi]

        def query_views(s):
            d = LAYERS[s.L]["d"]
            q = qf[s.j][:, :, :].rearrange("p t c -> p (t c)")[:, 0:T * H * d].rearrange("p (h d) -> p h d", d=d)
            return q, qs[LAYERS[s.L]["W"]][s.j], d

        def act_heads(s):
            HB = LAYERS[s.L]["HB"]
            return range(HB - 1, HB) if s.kind == "P3" else range(HB // 2, HB)

        def transposing(s):
            return (s.kind == "P3" and s.q > 0) or (s.kind == "N" and s.q % 2 == 1)

        def groups_of(s):
            half = s.q - 1 if s.kind == "P3" else s.q // 2
            n = H // LAYERS[s.L]["HB"] // 2
            return range(half * n, half * n + n)

        def block_views(s, groups, a, m):
            L = LAYERS[s.L]
            lo, hi = L["W"] * a, L["W"] * a + (L["W"] if s.kind == "P3" else MS)
            view = qblk[s.L][s.j][:, :, :].rearrange("p (g a) s -> p g a s", a=L["HB"])
            n = len(groups)
            return (view[lo:hi, groups[0]:groups[0] + n, a, :],
                    bf(m)[lo:hi, 0:n * S].rearrange("p (g s) -> p g s", g=n))

        def bf(m):
            return psM[:, m, :].bitcast(BF16)

        presets = [0]
        block = ctx.enter_context(nc.Block())

        @block.sync
        def _(sp):
            def load_x(pair, j):
                sp.dma_start(x[j][:, :, :], x_in[pair * 2 + j].rearrange("(t p) d -> p t d", p=128)).then_inc(x_loaded[j], 16)

            def load_context(pair):
                sp.dma_start(ctxk[:, :, :], ctx_in[:, pair, :, :]).then_inc(ctx_loaded, 16)
                for a in range(2):
                    sp.dma_start(ctxp[:, :, a, :], ctx_in[:, pair, :, :]).then_inc(ctx_loaded, 16)

            def store(pair, s):
                sp.wait_ge(a_drained, value(pair, "a_drained", s.a + 1))
                sp.dma_start(out[pair * 2 + s.j].rearrange("(t p) d -> p t d", p=128), yout[s.j][:, :, :]).then_inc(stored[s.j], 16)

            early_w, early_r = W_AT["win"][0], R_AT["bout"][0]
            sp.dma_start(W[:, 0:early_w], w_in[:, 0:early_w]).then_inc(early_loaded, 16)
            sp.dma_start(rows[:, 0:early_r], rows_in[0:early_r].partition_broadcast(128)).then_inc(early_loaded, 16)
            sp.dma_start(W[:, early_w:W_N], w_in[:, early_w:W_N]).then_inc(weights_loaded, 16)
            sp.dma_start(rows[:, early_r:R_N], rows_in[early_r:R_N].partition_broadcast(128)).then_inc(weights_loaded, 16)
            sp.dma_start(rope[:, :], rope_in).then_inc(weights_loaded, 16)
            sp.dma_start(wc[:, :], wc_in).then_inc(weights_loaded, 16)
            sp.dma_start(y2[0][:, 0:128], flip_in).then_inc(flip_loaded, 16)
            for j in range(2):
                load_x(0, j)
            load_context(0)
            sp.wait_ge(presets_done, 1)
            sp.dma_start(decay[:, 0:128], y1[0][0:NS, 0:128]).then_inc(decay_stored, 16)
            sp.wait_ge(decay_row, NS // 2)
            sp.dma_start(decay[:, 128:128 + S].unsqueeze(0), P[0:1, :, :, :].rearrange("p a b s -> p (a b) s")).then_inc(decay_stored, 16)
            sp.wait_ge(decay_stored, 32)
            for n in range(4):
                sp.dma_start(toep[:, 4 * n:4 * n + 4, :],
                             bass.AP(decay.tensor, 1 + 4 * n * (128 + S), [[1, 128], [128 + S, 4], [1, S]])).then_inc(toep_loaded[n], 16)

            context_used = next(s for s in steps if (s.kind, s.L, s.q) == ("C", "x1", 0))
            ends = [s for s in steps if s.kind == "H" and s.L == "f"]
            with sp.Fori(0, PAIRS - 1) as pair:
                m, _, _, c = context_used.misc["m"]
                sp.wait_ge(misc_drained[m], value(pair, f"misc_drained{m}", c))
                load_context(pair + 1)
                for s in ends:
                    store(pair, s)
                    load_x(pair + 1, s.j)
            for s in ends:
                store(PAIRS - 1, s)
            for j in range(2):
                sp.wait_ge(stored[j], value(PAIRS, f"stored{j}", 0))

        @block.gpsimd
        def _(pool):
            pool.memset(minus_half[:, :], -0.5).then_inc(eps_set, 1)
            pool.memset(ln_eps[:, :], LN_EPS).then_inc(eps_set, 1)
            pool.memset(rms_eps[:, :], RMS_EPS).then_inc(eps_set, 1)
            pool.memset(zero[:, :], 0.0).then_inc(eps_set, 1)
            pool.wait_ge(eps_set, 4)
            def preset(ap, v):
                presets[0] += 1
                pool.memset(ap, v).then_inc(presets_done, 1)

            preset(y1[0][:, :], 0.0)
            for j in range(2):
                for t in (qs[32][j], ks["s0"][j], ks["s1"][j], kblk["x0"][j], kblk["x1"][j], vx["x0"][j], vx["x1"][j], on4[j], gate[j]):
                    preset(t[:, :, :], 0.0)
                for t in (vp["s0"][j], vp["s1"][j]):
                    preset(t[:, :], 0.0)
            for t in (bdiag[0], kx["x0"], kx["x1"]):
                preset(t[:, :, :], 0.0)
            pool.wait_ge(presets_done, presets[0])
            for j in range(2):
                for t in (ks["s0"][j], ks["s1"][j]):
                    preset(t[:, :, 0:MS], 1.0)
                for half in range(2):
                    preset(value_view(vp["s0"][j], 4, half, DEN, DEN + 1), 1.0)
                    preset(value_view(vp["s1"][j], 2, half, DEN, DEN + 1), 1.0)
            for t in (kx["x0"], kx["x1"]):
                preset(t[:, :, 0:MS], 1.0)
            for half in range(2):
                pool.wait_ge(presets_done, presets[0])
                for j in range(2):
                    for name in ("x0", "x1"):
                        lo = 16 * half + DEN
                        preset(vx[name][j][64 * half:64 * half + 64, :, lo:lo + 1], 1.0)
            pool.wait_ge(presets_done, presets[0])
            for n, s in enumerate((a_drained, b_drained, p_used, a_filled, misc_drained[0], misc_drained[1],
                                   ot_drained[0], ot_drained[1], stored[0], stored[1])):
                pool.memset(tokens[:, n:n + 1], 0.0).then_inc(s, tuple(PRIME.values())[n])

            with pool.Fori(0, PAIRS) as pair:
                done = [0]

                def mark(ins):
                    done[0] += 1
                    ins.then_inc(pool_step, 1)

                def settle():
                    pool.wait_ge(pool_step, value(pair, "pool_step", done[0]))

                def split(src, tile, d, which, rest):
                    n = src.shape[1]
                    p1, p2, p3 = (parts(tile, d, w) for w in which)
                    a = src.unsqueeze(2)
                    nought = zero[:, :].unsqueeze(2).unsqueeze(3).broadcast_to([128, n, 3, d])
                    mark(pool.tensor_tensor(p1, a.broadcast_to([128, n, 3, d]), nought, ALU.subtract))
                    settle()
                    mark(pool.tensor_tensor(rest, src, p1[:, :, 0, :], ALU.subtract))
                    mark(pool.tensor_tensor(p2, a.broadcast_to([128, n, 2, d]), p1[:, :, 0:2, :], ALU.subtract))
                    settle()
                    return pool.tensor_tensor(p3[:, :, 0, :], rest, p2[:, :, 0, :], ALU.subtract)

                for s in steps:
                    j = s.j
                    d = LAYERS[s.L]["d"] if s.L in LAYERS else 0
                    if s.kind in ("T1", "P1") and s.q < norms(s.L):
                        pool.wait_ge(stats_ready, value(pair, "stats_ready", s.after["stats_ready"]))
                        rms = s.L == "s1" and s.q == 1
                        mark(pool.tensor_tensor(veps[j][:, :], ms[j][:, :] if rms else mv[j][:, :, 1],
                                                (rms_eps if rms else ln_eps)[:, :], ALU.add))
                        settle()
                        pool.tensor_tensor(rstd[j][:, :], veps[j][:, :], minus_half[:, :], ALU.pow).then_inc(rstd_ready, 1)
                    if s.kind == "C" and s.q == 0:
                        if s.L == "x0":
                            m, f, b, c = s.misc["m"]
                            pool.wait_ge(misc_drained[m], value(pair, f"misc_drained{m}", c))
                            n = 16
                        else:
                            pool.wait_ge(qk_ready, value(pair, "qk_ready", s.after["qk_ready"]))
                            n = 8
                        v = lambda t: t[:, 0:8 * n].rearrange("p (h d) -> p h d", d=8)
                        split(v(ckf), kx[s.L], d, K_PARTS, v(cres)).then_inc(k_split, 1)
                    if s.kind == "P3" and s.q == 0 and s.L in ks:
                        m, f, b, c = find(steps, "P2", s).misc["m"]
                        pool.wait_ge(misc_drained[m], value(pair, f"misc_drained{m}", c))
                        v = lambda t: t.rearrange("p (h d) -> p h d", d=d)
                        nk = T * (H if s.L == "s0" else 4) * d
                        split(v(kf[j][:, :, :].rearrange("p t c -> p (t c)")[:, 0:nk]), ks[s.L][j], d, K_PARTS,
                              v(kres[j][:, 0:nk])).then_inc(k_split, 1)
                    if s.kind == "T6":
                        mark(pool.tensor_tensor(base[j][:, :, :], x[j][:, :, :], xn[j][:, :, :], ALU.add))
                        settle()
                        pool.tensor_tensor(base[j][:, :, :], base[j][:, :, :],
                                           row("bout").unsqueeze(1).broadcast_to([128, T, D]), ALU.add).then_inc(base_ready, 1)
                    if s.kind == "F3" and s.L != "s0":
                        if s.L == "s1":
                            m, f, b, c = find(steps, "F1", s).misc["m"]
                            pool.wait_ge(misc_drained[m], value(pair, f"misc_drained{m}", c))
                            other = on[j][:, :, :]
                        else:
                            other = row(s.L + "bo").unsqueeze(1).broadcast_to([128, T, D])
                        pool.tensor_tensor(base[j][:, :, :], x[j][:, :, :], other, ALU.add).then_inc(base_ready, 1)
                    if s.kind == "R3":
                        pool.tensor_tensor(base[j][:, :, :], x[j][:, :, :], xn[j][:, :, :], ALU.add).then_inc(base_ready, 1)
                    if s.kind == "H" and s.L == "f":
                        pool.tensor_tensor(base[j][:, :, :], x[j][:, :, :],
                                           row("fb2").unsqueeze(1).broadcast_to([128, T, D]), ALU.add).then_inc(base_ready, 1)
                assert done[0] == POOL_STEPS, done[0]

        @block.scalar
        def _(act):
            act.wait_ge(early_loaded, 32)
            act.dma_start(w1[:, :], w1_in).then_inc(weights2_loaded, 16)
            act.dma_start(w2[:, :], w2_in).then_inc(weights2_loaded, 16)
            act.dma_start(b2[:, :], b2_in).then_inc(weights2_loaded, 16)
            act.dma_start(fw1[:, :], fw1_in).then_inc(weights2_loaded, 16)
            act.dma_start(fw2[:, :], fw2_in).then_inc(weights2_loaded, 16)
            act.activation(dt[:, 0:1], wc_("logdt"), ACT.Exp).then_inc(decay_terms, 1)
            act.activation(xm[0][:, 0:NS], wc_("alog"), ACT.Exp).then_inc(decay_terms, 1)
            act.wait_ge(logs_ready, 1)
            for s_ in range(NS):
                act.activation(toep[:, s_, :], row("iota"), ACT.Exp, scale=xm[1][:, s_:s_ + 1]).then_inc(decay_terms, 1)

            act.wait_ge(half_bias_ready, 1)
            act.wait_ge(weights_loaded, 64)
            act.wait_ge(blocks_blank, 6)
            with act.Fori(0, PAIRS) as pair:
                def free(s, name):
                    m, f, b, c = s.misc[name]
                    act.wait_ge(misc_filled[m], value(pair, f"misc_filled{m}", f))
                    return m

                def claim(s, n):
                    name, count = p_release[s.b + n]
                    act.wait_ge(sems[name], value(pair, name, count))
                    act.wait_ge(b_filled, value(pair, "b_filled", s.b + n + 1))
                    return s.p[n]

                for s in steps:
                    j = s.j
                    if s.kind in ("T1", "P1") and s.q == norms(s.L):
                        m = free(s, "m")
                        if s.kind == "T1":
                            act.activation(xnT[j][:, :], psM[:, m, 0:S], ACT.Identity, bias=wc_("lnb"), scale=wc_("lng")).then_inc(misc_drained[m], 1)
                        elif s.L == "s1":
                            act.activation(xnT[j][:, :], psM[:, m, 0:S], ACT.Identity, scale=wc_("rmsg")).then_inc(misc_drained[m], 1)
                        else:
                            act.copy(xnT[j][:, :], psM[:, m, 0:S]).then_inc(misc_drained[m], 1)
                    if s.kind == "T2":
                        m = free(s, "m")
                        act.activation(xpT[j][:, :], psM[:, m, 0:S], ACT.Identity, bias=wc_("bx"))
                        act.activation(zs[j][:, :], psM[:, m, S:2 * S], ACT.Identity, bias=wc_("bz"))
                        act.activation(zt[j][:, :], psM[:, m, S:2 * S], ACT.Tanh, bias=dt[:, 3:4], scale=0.5).then_inc(misc_drained[m], 1)
                    if s.kind == "T4":
                        m = free(s, "m")
                        act.copy(xm[j][:, :], psM[:, m, 0:S]).then_inc(misc_drained[m], 1)
                    if s.kind == "P3" and s.q == 0:
                        p2 = find(steps, "P2", s)
                        if s.L == "x1":
                            act.wait_ge(qk_ready, value(pair, "qk_ready", p2.after["qk_ready"]))
                        else:
                            m, f, b, c = p2.misc["m"]
                            act.wait_ge(misc_drained[m], value(pair, f"misc_drained{m}", c))
                        q, tile, d = query_views(s)
                        act.copy(parts(tile, d, Q_PARTS[0]), q.unsqueeze(2).broadcast_to([128, T * H, 3, d])).then_inc(q_part1, 1)
                    if transposing(s) and not LAYERS[s.L]["cross"]:
                        L = LAYERS[s.L]
                        if "k" in s.misc:
                            m = free(s, "k")
                            KG = L["KG"]
                            act.copy(KT[j][:, 0:KG, :], bf(m)[:, 0:KG * S]).then_inc(misc_drained[m], 1)
                        m = free(s, "m")
                        for a in act_heads(s):
                            dst, src = block_views(s, groups_of(s), a, m)
                            ins = act.copy(dst, src)
                        ins.then_inc(misc_drained[m], 1)
                    if s.kind == "S":
                        for n in range(units(s)[1]):
                            p = claim(s, n)
                            act.activation(P[:, p, :, :].rearrange("p a s -> p (a s)"), psB[:, (s.b + n) % B_BANKS, :], ACT.Exp,
                                           scale=LAYERS[s.L]["scale"]).then_inc(b_drained, 1)
                    if s.kind == "G":
                        p = claim(s, 0)
                        bias = wc_("b1") if s.L == "s0" else wc_("fb1")
                        for f in range(2):
                            n = 2 * s.q + f
                            ins = act.activation(P[:, p, f, :], psB[:, s.b % B_BANKS, f * S:f * S + S], ACT.Gelu, bias=bias[:, n:n + 1])
                        ins.then_inc(b_drained, 1)
                    if s.kind == "F1":
                        v = find(steps, "V", s)
                        act.wait_ge(p_used, value(pair, "p_used", v.after["p_used"]))
                        act.copy(ots[j][:, :, :].rearrange("p u s -> p (u s)"), psO[:, j, :, :].rearrange("p u s -> p (u s)")).then_inc(ot_drained[j], 1)
                    if s.kind == "F2":
                        m = free(s, "m")
                        act.copy(onT[j][:, :], psM[:, m, 0:S]).then_inc(misc_drained[m], 1)
                    if s.kind == "F3" and s.L == "s0":
                        m = free(s, "m")
                        act.activation(mlaT[j][:, :], psM[:, m, 0:S], ACT.Identity, bias=wc_("mlab")).then_inc(misc_drained[m], 1)
                    if s.kind == "R1" and s.q == 0:
                        act.wait_ge(logits_ready, value(pair, "logits_ready", s.after["logits_ready"]))
                        act.activation(lexp[j][:, :, :], lg[j][:, :, :], ACT.Exp).then_inc(router_exp, 1)
                    if s.kind == "R2":
                        m = free(s, "m")
                        act.copy(gateT[j][:, :], psM[:, m, 0:S]).then_inc(misc_drained[m], 1)

        @block.vector
        def _(dve):
            for j in range(2):
                for t in (qs[64][j], qblk["s0"][j], qblk["s1"][j]):
                    dve.memset(t[:, :, :], 0.0).then_inc(blocks_blank, 1)
            dve.wait_ge(early_loaded, 32)
            dve.tensor_copy(identb[:, :], wc_("ident")).then_inc(ident_ready, 1)
            dve.wait_ge(decay_terms, 2)
            dve.tensor_scalar(dt[:, 1:2], dt[:, 0:1], 1e-4, 1.0, ALU.max, ALU.min).then_inc(dt_clipped, 1)
            dve.wait_ge(dt_clipped, 1)
            dve.tensor_scalar(xm[1][:, 0:NS], xm[0][:, 0:NS], dt[:, 1:2], -1.0, ALU.mult, ALU.mult).then_inc(rates_ready, 1)
            dve.wait_ge(rates_ready, 1)
            dve.tensor_scalar(xm[1][:, 0:NS], xm[1][:, 0:NS], float(np.log(1e-8)), float(np.log1p(-1e-8)), ALU.max, ALU.min).then_inc(logs_ready, 1)
            dve.tensor_scalar(dt[:, 3:4], wc_("bz"), 0.5, None, ALU.mult).then_inc(half_bias_ready, 1)
            dve.wait_ge(dt_sum, 1)
            dve.tensor_copy(dt[:, 2:3], psM[:, 0, 0:1]).then_inc(dt_mean, 1)
            for n in range(NS // 2):
                dve.wait_ge(decay_mean, n + 1)
                dve.tensor_copy(P[0:1, n, :, :].rearrange("p a s -> p (a s)"), psB[0:1, n % 2, :]).then_inc(decay_row, 1)
            for n in range(NS // 2):
                dve.wait_ge(toep_flipped, n + 1)
                dve.tensor_copy(toep[:, 2 * n:2 * n + 2, :].rearrange("p a s -> p (a s)"), psB[:, n % 2, :]).then_inc(toep_ready, 1)
            dve.wait_ge(presets_done, presets[0])
            dve.wait_ge(blocks_blank, 6)
            dve.wait_ge(weights_loaded, 64)

            with dve.Fori(0, PAIRS) as pair:
                done = [0]

                def mark(ins):
                    done[0] += 1
                    ins.then_inc(dve_step, 1)

                def settle():
                    dve.wait_ge(dve_step, value(pair, "dve_step", done[0]))

                def filled(s, name="m"):
                    m, f, b, c = s.misc[name]
                    dve.wait_ge(misc_filled[m], value(pair, f"misc_filled{m}", f))
                    return m

                def drained(s, name="m"):
                    m, f, b, c = s.misc[name]
                    dve.wait_ge(misc_drained[m], value(pair, f"misc_drained{m}", c))

                def moments(s, src, j, rms=False):
                    for t in range(T):
                        mark(dve.bn_stats(stats[j][:, t, :], src[:, t, :]))
                    settle()
                    dve.memset(wait_carrier[:, :], 0.0)
                    for t in range(T):
                        ins = dve.bn_aggr(mv[j][:, t, :], stats[j][:, t, :])
                        if rms or t == 0:
                            mark(ins)
                    if not rms:
                        ins.then_inc(stats_ready, 1)
                        return
                    settle()
                    mark(dve.tensor_tensor(ms[j][:, :], mv[j][:, :, 0], mv[j][:, :, 0], ALU.mult))
                    settle()
                    dve.tensor_tensor(ms[j][:, :], ms[j][:, :], mv[j][:, :, 1], ALU.add).then_inc(stats_ready, 1)

                def normalise(s, src, dst, j, final, rms=False):
                    dve.wait_ge(rstd_ready, value(pair, "rstd_ready", find(steps, s.kind, s, s.q - 1).after["rstd_ready"]))
                    for t in range(T):
                        if rms:
                            ins = dve.tensor_scalar(dst[:, t, :], src[:, t, :], rstd[j][:, t:t + 1], None, ALU.mult)
                        else:
                            ins = dve.tensor_scalar(dst[:, t, :], src[:, t, :], mv[j][:, t, 0:1], rstd[j][:, t:t + 1],
                                                    ALU.subtract, ALU.mult)
                        if not (final and t == T - 1):
                            mark(ins)
                    if final:
                        ins.then_inc(xn_ready, 1)

                prev = {0: None, 1: None}
                for s in steps:
                    j = s.j
                    L = LAYERS.get(s.L)
                    d = L["d"] if L else 0
                    if s.kind in ("T1", "P1"):
                        if s.q == 0:
                            if s.kind == "T1":
                                dve.wait_ge(x_loaded[j], value(pair, f"x_loaded{j}", 16))
                            elif prev[j].kind == "H":
                                dve.wait_ge(a_drained, value(pair, "a_drained", prev[j].a + 1))
                            else:
                                drained(prev[j], "m")
                            moments(s, x[j], j)
                        if s.q == 1:
                            normalise(s, x[j], xn[j], j, norms(s.L) == 1)
                            if norms(s.L) == 2:
                                settle()
                                moments(s, xn[j], j, rms=s.L == "s1")
                        if s.q == 2:
                            normalise(s, xn[j], xn2[j], j, True, rms=s.L == "s1")
                    if s.kind == "T3":
                        m = filled(s)
                        if j == 0:
                            dve.wait_ge(dt_mean, 1)
                        dve.tensor_scalar(bdiag[j][:, :, 0:NS * 33:33], psM[:, m, 0:T * NS].rearrange("p (t s) -> p t s", t=T),
                                          dt[:, 2:3], None, ALU.mult).then_inc(misc_drained[m], 1)
                    if s.kind == "T5":
                        mark(dve.scalar_tensor_tensor(y2[j][:, :], zt[j][:, :], 1.0, zs[j][:, :], ALU.add, ALU.mult))
                        m = filled(s)
                        dve.scalar_tensor_tensor(y1[j][:, :], xpT[j][:, :], wc_("dskip"), psM[:, m, 0:S],
                                                 ALU.mult, ALU.add).then_inc(misc_drained[m], 1)
                        drained(s)
                        dve.scalar_tensor_tensor(y2[j][:, :], y1[j][:, :], 0.5, y2[j][:, :], ALU.mult, ALU.mult).then_inc(y_ready, 1)
                    if s.kind == "T6" or (s.kind == "F3" and s.L != "s0"):
                        m = filled(s)
                        dve.wait_ge(base_ready, value(pair, "base_ready", s.after["base_ready"]))
                        dve.tensor_tensor(x[j][:, :, :].rearrange("p t d -> p (t d)"), psM[:, m, 0:S],
                                          base[j][:, :, :].rearrange("p t d -> p (t d)"), ALU.add).then_inc(misc_drained[m], 1)
                        prev[j] = s
                    if s.kind == "C" and s.q == 0:
                        m = filled(s)
                        ps = psM[:, m, :]
                        nk = 128 if s.L == "x0" else 32
                        for jj in range(2):
                            for a in range(2):
                                r = slice(64 * a, 64 * a + 64)
                                lo = nk + jj * nk
                                o = vx[s.L][jj][r, :, 16 * a:16 * a + 8]
                                if s.L == "x0":
                                    sel = lambda v: v.rearrange("p (h a d) -> p h a d", a=2, d=8)[:, :, a, :]
                                    mark(dve.tensor_tensor(o, sel(ps[r, lo:lo + nk]), sel(row("x0bv")[r, :]), ALU.add))
                                else:
                                    sel = lambda v: v.rearrange("p (g d) -> p g d", d=8).unsqueeze(2).broadcast_to([64, 4, 2, 8])
                                    mark(dve.tensor_tensor(o.rearrange("p (g r) d -> p g r d", r=2), sel(ps[r, lo:lo + nk]),
                                                           sel(row("x1bv")[r, :]), ALU.add))
                        if s.L == "x0":
                            dve.tensor_tensor(ckf[:, :], ps[:, 0:nk], row("x0bk"), ALU.add).then_inc(misc_drained[m], 1)
                        else:
                            dve.tensor_tensor(ck1[:, :], ps[:, 0:nk], row("x1bk"), ALU.add).then_inc(misc_drained[m], 1)
                            drained(s)
                            k3 = lambda t: t[:, :].rearrange("p (h d) -> p h d", d=8)
                            cs = lambda n, lo, hi: tab(n)[:, lo:hi].unsqueeze(1).broadcast_to([128, 4, hi - lo])
                            mark(dve.tensor_tensor(k3(ck2), k3(ck1), cs("kcos", 0, 8), ALU.mult))
                            mark(dve.tensor_tensor(k3(ck3)[:, :, 0:4], k3(ck1)[:, :, 4:8], cs("ksin", 0, 4), ALU.mult))
                            mark(dve.tensor_tensor(k3(ck3)[:, :, 4:8], k3(ck1)[:, :, 0:4], cs("ksin", 4, 8), ALU.mult))
                            settle()
                            wide = lambda t: k3(t).unsqueeze(2).broadcast_to([128, 4, 2, 8])
                            dve.tensor_tensor(ckf[:, 0:64].rearrange("p (g r d) -> p g r d", r=2, d=8), wide(ck2), wide(ck3),
                                              ALU.add).then_inc(qk_ready, 1)
                    if s.kind == "C" and s.q == 1:
                        m = filled(s)
                        n = L["KG"]
                        for jj in range(2):
                            for a in range(2):
                                r = slice(64 * a, 64 * a + 64)
                                ins = dve.tensor_copy(kblk[s.L][jj][r, :, 64 * a:64 * a + 64],
                                                      bf(m)[r, 0:n * 128].rearrange("p (g c) -> p g c", c=128)[:, :, 64 * jj:64 * jj + 64])
                                if (jj, a) != (1, 1):
                                    mark(ins)
                        ins.then_inc(misc_drained[m], 1)
                    if s.kind == "P2":
                        m = filled(s)
                        ps = psM[:, m, :]
                        flat = lambda t: t[:, :, :].rearrange("p t c -> p (t c)")
                        if s.L == "x0":
                            dve.tensor_tensor(flat(qf[j]), ps[:, 0:256], row("x0bq"), ALU.add).then_inc(misc_drained[m], 1)
                        elif s.L == "x1":
                            dve.tensor_tensor(flat(qt1[j]), ps[:, 0:256], row("x1bq"), ALU.add).then_inc(misc_drained[m], 1)
                            drained(s)
                            q4 = lambda t: t[:, :, :].rearrange("p t (h d) -> p t h d", d=8)
                            cs = lambda n, lo, hi: tab(n).rearrange("p (t d) -> p t d", d=8)[:, :, lo:hi].unsqueeze(2).broadcast_to([128, T, H, hi - lo])
                            mark(dve.tensor_tensor(q4(qt2[j])[:, :, :, 0:4], q4(qt1[j])[:, :, :, 4:8], cs("qsin", 0, 4), ALU.mult))
                            mark(dve.tensor_tensor(q4(qt2[j])[:, :, :, 4:8], q4(qt1[j])[:, :, :, 0:4], cs("qsin", 4, 8), ALU.mult))
                            mark(dve.tensor_tensor(q4(qf[j]), q4(qt1[j]), cs("qcos", 0, 8), ALU.mult))
                            settle()
                            dve.tensor_tensor(flat(qf[j]), flat(qf[j]), flat(qt2[j]), ALU.add).then_inc(qk_ready, 1)
                        elif s.L == "s0":
                            q = ps[:, 0:256].rearrange("p (t c) -> p t c", t=T)
                            fl = lambda t, n: flat(t)[:, 0:n].rearrange("p (t c) -> p t c", t=T)
                            mark(dve.tensor_tensor(fl(qf[j], 128), q[:, :, 0:64], row("s0bq").rearrange("p (t c) -> p t c", t=T), ALU.add))
                            mark(dve.tensor_tensor(fl(kf[j], 128), q[:, :, 64:128], row("s0bk").rearrange("p (t c) -> p t c", t=T), ALU.add))
                            for h in range(2):
                                vv = lambda v: v.rearrange("p (g h c d) -> p g h c d", h=2, c=4, d=4)[:, :, h, :, :]
                                o = value_view(vp["s0"][j], 4, h, 0, 4)
                                ins = dve.tensor_tensor(o, vv(ps[:, 256:384]), vv(row("s0bv")), ALU.add)
                                if h == 0:
                                    mark(ins)
                            ins.then_inc(misc_drained[m], 1)
                        else:
                            q = ps[:, 0:320].rearrange("p (t h d) -> p t h d", t=T, d=8)
                            rf = tab("rf").rearrange("p (t d) -> p t d", d=8).unsqueeze(2)
                            mark(dve.tensor_tensor(qf[j][:, :, :].rearrange("p t (h d) -> p t h d", d=8), q[:, :, 0:16, :],
                                                   rf.broadcast_to([128, T, 16, 8]), ALU.mult))
                            mark(dve.tensor_tensor(flat(kf[j])[:, 0:64].rearrange("p (t h d) -> p t h d", t=T, d=8), q[:, :, 16:20, :],
                                                   rf.broadcast_to([128, T, 4, 8]), ALU.mult))
                            for h in range(2):
                                o = value_view(vp["s1"][j], 2, h, 0, 8)
                                ins = dve.tensor_copy(o, ps[:, 320:384].rearrange("p (t c d) -> p t c d", t=T, d=8))
                                if h == 0:
                                    mark(ins)
                            ins.then_inc(misc_drained[m], 1)
                    if s.kind == "P3" and s.q == 0:
                        q, tile, _ = query_views(s)
                        p1, p2, p3 = (parts(tile, d, w) for w in Q_PARTS)
                        rest = qres[j][:, 0:T * H * d].rearrange("p (h d) -> p h d", d=d)
                        mark(dve.memset(tile[:, :, 0:MS], 0.0))
                        dve.wait_ge(q_part1, value(pair, "q_part1", s.after["q_part1"]))
                        mark(dve.tensor_tensor(p2, q.unsqueeze(2).broadcast_to([128, T * H, 2, d]), p1[:, :, 0:2, :], ALU.subtract))
                        mark(dve.tensor_tensor(rest, q, p1[:, :, 0, :], ALU.subtract))
                        settle()
                        dve.tensor_tensor(p3[:, :, 0, :], rest, p2[:, :, 0, :], ALU.subtract).then_inc(q_split, 1)
                    if s.kind == "N" and s.q % 2 == 0:
                        lo = s.q // 2 * (H // 2)
                        q = qs[L["W"]][j][:, :, :].rearrange("p (t h) w -> p t h w", t=T)[:, :, lo:lo + H // 2, :]
                        nm = nmax[j][:, :, lo:lo + H // 2]
                        last_a = find(steps, "A", s, s.q + 1)
                        dve.wait_ge(a_drained, value(pair, "a_drained", last_a.a + units(last_a)[0]))
                        mark(dve.tensor_copy(q[:, :, :, 0], nm))
                        settle()
                        dve.tensor_tensor(q[:, :, :, 1], nm, q[:, :, :, 0], ALU.subtract).then_inc(max_in_slots, 1)
                    if transposing(s):
                        m = filled(s)
                        groups = groups_of(s)
                        if L["cross"]:
                            dve.tensor_copy(QT[j][:, groups[0]:groups[0] + 4, :].rearrange("p g s -> p (g s)"), bf(m)).then_inc(misc_drained[m], 1)
                        else:
                            for a in range(act_heads(s)[0]):
                                dst, src = block_views(s, groups, a, m)
                                ins = dve.tensor_copy(dst, src)
                                if a + 1 < act_heads(s)[0]:
                                    mark(ins)
                            ins.then_inc(misc_drained[m], 1)
                    if s.kind == "A":
                        for n in range(units(s)[0]):
                            dve.wait_ge(a_filled, value(pair, "a_filled", s.a + n + 1))
                            ps = psA[:, (s.a + n) % A_BANKS, :]
                            if L["cross"]:
                                dve.tensor_reduce(nmax[j][:, :, 4 * s.q:4 * s.q + 4],
                                                  ps.rearrange("p (t h c) -> p t h c", t=T, c=C), AX.X, ALU.max,
                                                  negate=True).then_inc(a_drained, 1)
                            else:
                                h = 4 * s.q + n
                                dve.tensor_reduce(nmax[j][:, :, h], ps.rearrange("p (t c) -> p t c", t=T), AX.X, ALU.max,
                                                  negate=True).then_inc(a_drained, 1)
                    if s.kind == "F1":
                        m = filled(s)
                        ps = psM[:, m, :].rearrange("p (n e) -> p n e", e=16)
                        mark(dve.reciprocal(rden[j][:, :], ps[:, :, DEN]))
                        settle()
                        o = on4[j] if s.L == "s0" else on[j]
                        if L["cross"]:
                            dve.tensor_tensor(o[:, :, :].rearrange("p t (h d) -> p (t h) d", d=8), ps[:, :, 0:8],
                                              rden[j][:, :].unsqueeze(2).broadcast_to([128, 32, 8]), ALU.mult).then_inc(misc_drained[m], 1)
                        else:
                            for n in range(4):
                                t, u = n // 2, n % 2
                                oo = o[:, t, 8 * u * d:8 * u * d + 8 * d].rearrange("p (b c d) -> p c b d", b=2, d=d)
                                ii = ps[:, 8 * n:8 * n + 8, 0:d].rearrange("p (c b) d -> p c b d", b=2)
                                rr = rden[j][:, 8 * n:8 * n + 8].rearrange("p (c b) -> p c b", b=2).unsqueeze(3).broadcast_to([128, 4, 2, d])
                                ins = dve.tensor_tensor(oo, ii, rr, ALU.mult)
                                if n < 3:
                                    mark(ins)
                            ins.then_inc(misc_drained[m], 1)
                    if s.kind == "R1" and s.q == 0:
                        m = filled(s)
                        dve.tensor_tensor(lg[j][:, :, :].rearrange("p t e -> p (t e)"), psM[:, m, 0:T * E], row("rb"), ALU.add).then_inc(misc_drained[m], 1)
                        drained(s)
                        mark(dve.tensor_reduce(lmax[j][:, :], lg[j][:, :, :], AX.X, ALU.max))
                        settle()
                        bc = lambda v: v[:, :].unsqueeze(2).broadcast_to([128, T, E])
                        dve.tensor_tensor(lg[j][:, :, :], lg[j][:, :, :], bc(lmax[j]), ALU.subtract).then_inc(logits_ready, 1)
                    if s.kind == "R1" and s.q == 1:
                        bc = lambda v: v[:, :].unsqueeze(2).broadcast_to([128, T, E])
                        dve.wait_ge(router_exp, value(pair, "router_exp", s.after["router_exp"]))
                        mark(dve.tensor_reduce(gsum[j][:, :], lexp[j][:, :, :], AX.X, ALU.add))
                        settle()
                        mark(dve.reciprocal(gsum[j][:, :], gsum[j][:, :]))
                        settle()
                        p3 = prob[j][:, :].rearrange("p (t e) -> p t e", e=E)
                        mark(dve.tensor_tensor(p3, lexp[j][:, :, :], bc(gsum[j]), ALU.mult))
                        settle()
                        c4 = lambda v: v[:, :].rearrange("p (t e f) -> p t e f", e=E, f=E)
                        others = p3.unsqueeze(2).broadcast_to([128, T, E, E])
                        mine4 = p3.unsqueeze(3).broadcast_to([128, T, E, E])
                        mark(dve.tensor_tensor(c4(above[j]), others, mine4, ALU.is_gt))
                        mark(dve.tensor_tensor(c4(ties[j]), others, mine4, ALU.is_equal))
                        settle()
                        mark(dve.tensor_tensor(ties[j][:, :], ties[j][:, :], row("tri"), ALU.mult))
                        settle()
                        mark(dve.tensor_tensor(above[j][:, :], above[j][:, :], ties[j][:, :], ALU.add))
                        settle()
                        mark(dve.tensor_reduce(rank[j][:, :], above[j][:, :].rearrange("p (n f) -> p n f", f=E), AX.X, ALU.add))
                        settle()
                        mark(dve.scalar_tensor_tensor(rank[j][:, :], rank[j][:, :], 2.0, prob[j][:, :], ALU.is_lt, ALU.mult))
                        settle()
                        r3 = rank[j][:, :].rearrange("p (t e) -> p t e", e=E)
                        mark(dve.tensor_reduce(gsum[j][:, :], r3, AX.X, ALU.add))
                        settle()
                        mark(dve.tensor_scalar(gsum[j][:, :], gsum[j][:, :], 1e-8, None, ALU.add))
                        settle()
                        mark(dve.reciprocal(gsum[j][:, :], gsum[j][:, :]))
                        settle()
                        dve.scalar_tensor_tensor(gate[j][:, :, 0:E], r3, 0.3, bc(gsum[j]), ALU.mult, ALU.mult).then_inc(gates_ready, 1)
                    if s.kind == "R3":
                        m = filled(s)
                        dve.wait_ge(base_ready, value(pair, "base_ready", s.after["base_ready"]))
                        dve.tensor_tensor(x[j][:, :, :].rearrange("p t d -> p (t d)"), psM[:, m, 0:S],
                                          base[j][:, :, :].rearrange("p t d -> p (t d)"), ALU.add).then_inc(misc_drained[m], 1)
                        prev[j] = s
                    if s.kind == "H":
                        dve.wait_ge(a_filled, value(pair, "a_filled", s.a + 1))
                        ps = psA[:, s.a % A_BANKS, :]
                        if s.L == "s0":
                            if prev[j].kind == "R3":
                                drained(prev[j])
                            else:
                                dve.wait_ge(a_drained, value(pair, "a_drained", prev[j].a + 1))
                            for t in range(T):
                                ins = dve.scalar_tensor_tensor(x[j][:, t, :], ps[:, t * D:t * D + D], gate[j][:, t, s.q:s.q + 1],
                                                               x[j][:, t, :], ALU.mult, ALU.add)
                                if t == 0:
                                    mark(ins)
                            ins.then_inc(a_drained, 1)
                            prev[j] = s
                        else:
                            dve.wait_ge(base_ready, value(pair, "base_ready", s.after["base_ready"]))
                            dve.wait_ge(stored[j], value(pair, f"stored{j}", 0))
                            dve.tensor_tensor(yout[j][:, :, :].rearrange("p t d -> p (t d)"), ps[:, 0:S],
                                              base[j][:, :, :].rearrange("p t d -> p (t d)"), ALU.add).then_inc(a_drained, 1)
                assert done[0] == DVE_STEPS, done[0]

        @block.tensor
        def _(pe):
            pe.wait_ge(early_loaded, 32)
            pe.wait_ge(ident_ready, 1)
            pe.wait_ge(dt_clipped, 1)
            pe.matmul(psM[:, 0, 0:1], wc_("ones"), dt[:, 1:2], start=True, stop=True).then_inc(dt_sum, 1)
            for n in range(NS // 2):
                pe.wait_ge(decay_terms, 2 + 2 * n + 2)
                if n >= 2:
                    pe.wait_ge(decay_row, n - 1)
                pe.matmul(psB[0:1, n % 2, :], wc_("ones")[:, 0:1], toep[:, 2 * n:2 * n + 2, :].rearrange("p a s -> p (a s)"),
                          start=True, stop=True).then_inc(decay_mean, 1)
            pe.wait_ge(decay_row, NS // 2)
            pe.wait_ge(dt_mean, 1)
            pe.wait_ge(flip_loaded, 16)
            for n in range(NS // 2):
                if n % 2 == 0:
                    pe.wait_ge(toep_loaded[n // 2], 16)
                if n >= 2:
                    pe.wait_ge(toep_ready, n - 1)
                pe.matmul(psB[:, n % 2, :], y2[0][:, 0:128], toep[:, 2 * n:2 * n + 2, :].rearrange("p a s -> p (a s)"),
                          start=True, stop=True).then_inc(toep_flipped, 1)
            pe.wait_ge(toep_ready, NS // 2)
            pe.wait_ge(presets_done, presets[0])
            pe.wait_ge(blocks_blank, 6)
            pe.wait_ge(weights_loaded, 64)
            pe.wait_ge(weights2_loaded, 80)

            with pe.Fori(0, PAIRS) as pair:
                def take(s, name="m"):
                    m, f, b, c = s.misc[name]
                    pe.wait_ge(misc_drained[m], value(pair, f"misc_drained{m}", b))
                    return m

                def drained(s, name="m"):
                    m, f, b, c = s.misc[name]
                    pe.wait_ge(misc_drained[m], value(pair, f"misc_drained{m}", c))

                def reuse(name, unit, banks):
                    last = unit - banks
                    if last < 0:
                        last = max(k for k in range(total[name]) if k % banks == unit % banks) - total[name]
                    pe.wait_ge(sems[name], value(pair, name, last + 1))

                def to_columns(m, src):
                    for t in range(T):
                        ins = pe.transpose(psM[:, m, t * 128:t * 128 + 128], src[:, t, :], wc_("ident"))
                    return ins

                for s in steps:
                    j = s.j
                    L = LAYERS.get(s.L)
                    if s.kind in ("T1", "P1") and s.q == norms(s.L):
                        m = take(s)
                        pe.wait_ge(xn_ready, value(pair, "xn_ready", s.after["xn_ready"]))
                        src = xn2[j] if s.kind == "T1" or s.L == "s1" else xn[j]
                        to_columns(m, src).then_inc(misc_filled[m], 1)
                    if s.kind == "T2":
                        drained(find(steps, "T1", s))
                        m = take(s)
                        for n in range(2):
                            ins = pe.matmul(psM[:, m, n * S:n * S + S], wc_("win")[:, n * D:n * D + D], xnT[j][:, :], start=True, stop=True)
                        ins.then_inc(misc_filled[m], 1)
                    if s.kind == "T3":
                        drained(find(steps, "T2", s))
                        m = take(s)
                        for t in range(T):
                            ins = pe.matmul(psM[:, m, t * NS:t * NS + NS], xpT[j][:, t * 128:t * 128 + 128], wc_("wb"), start=True, stop=True)
                        ins.then_inc(misc_filled[m], 1)
                    if s.kind == "T4":
                        drained(find(steps, "T3", s))
                        m = take(s)
                        for n in range(NS // 4):
                            for t in range(T):
                                for c in range(4):
                                    st = 4 * n + c
                                    ins = pe.matmul(psM[32 * c:32 * c + 32, m, t * 128:S], bdiag[j][:, t, st * 32:st * 32 + 32],
                                                    toep[:, st, 0:S - t * 128], start=(n == 0 and t == 0), stop=(n == 3 and t == 1),
                                                    skip_group_check=True)
                        ins.then_inc(misc_filled[m], 1)
                    if s.kind == "T5":
                        drained(find(steps, "T4", s))
                        m = take(s)
                        pe.matmul(psM[:, m, 0:S], wc[:, :], xm[j][:, :], start=True, stop=True).then_inc(misc_filled[m], 1)
                    if s.kind == "T6":
                        pe.wait_ge(y_ready, value(pair, "y_ready", s.after["y_ready"]))
                        m = take(s)
                        for t in range(T):
                            ins = pe.matmul(psM[:, m, t * D:t * D + D], y2[j][:, t * 128:t * 128 + 128], wc_("wout"), start=True, stop=True)
                        ins.then_inc(misc_filled[m], 1)
                    if s.kind == "C" and s.q == 0:
                        if s.L == "x0":
                            pe.wait_ge(ctx_loaded, value(pair, "ctx_loaded", 48))
                        m = take(s)
                        nk = 128 if s.L == "x0" else 32
                        pe.matmul(psM[:, m, 0:nk], ctxk[:, :, :], wc_(s.L + "k"), start=True, stop=True)
                        for jj in range(2):
                            lo = nk + jj * nk
                            ins = pe.matmul(psM[:, m, lo:lo + nk], ctxp[:, jj, :, :], wc_(s.L + "v"), start=True, stop=True)
                        ins.then_inc(misc_filled[m], 1)
                    if s.kind == "C" and s.q == 1:
                        m = take(s)
                        pe.wait_ge(k_split, value(pair, "k_split", find(steps, "C", s, 0).after["k_split"]))
                        for g in range(L["KG"]):
                            ins = pe.transpose(bf(m)[:, g * 128:g * 128 + 128], kx[s.L][:, 2 * g:2 * g + 2, :], identb[:, :])
                        ins.then_inc(misc_filled[m], 1)
                    if s.kind == "P2":
                        drained(find(steps, "P1", s))
                        m = take(s)
                        lhs = [xnT[j][:, t * 128:t * 128 + 128] for t in range(T)]
                        if L["cross"]:
                            for t in range(T):
                                ins = pe.matmul(psM[:, m, t * D:t * D + D], lhs[t], wc_(s.L + "q"), start=True, stop=True)
                        else:
                            n = 128 if s.L == "s0" else 160
                            nv = 64 if s.L == "s0" else 32
                            for t in range(T):
                                pe.matmul(psM[:, m, t * n:t * n + n], lhs[t], wc_(s.L + "qk"), start=True, stop=True)
                            for t in range(T):
                                lo = T * n + t * nv
                                ins = pe.matmul(psM[:, m, lo:lo + nv], lhs[t], wc_(s.L + "v"), start=True, stop=True)
                        ins.then_inc(misc_filled[m], 1)
                    if transposing(s):
                        HB, KG = L["HB"], L["KG"]
                        if "k" in s.misc:
                            m = take(s, "k")
                            pe.wait_ge(k_split, value(pair, "k_split", find(steps, "P3", s, 0).after["k_split"]))
                            nh = T * H if s.L == "s0" else T * 4
                            for g in range(KG):
                                for t in range(T):
                                    h = t * nh // 2 + g * HB
                                    ins = pe.transpose(bf(m)[:, g * S + t * 128:g * S + t * 128 + 128],
                                                       ks[s.L][j][:, h:h + HB, :], identb[:, :])
                            ins.then_inc(misc_filled[m], 1)
                        if s.kind == "P3":
                            pe.wait_ge(q_split, value(pair, "q_split", find(steps, "P3", s, 0).after["q_split"]))
                        else:
                            n0 = find(steps, "N", s, s.q - 1)
                            pe.wait_ge(max_in_slots, value(pair, "max_in_slots", n0.after["max_in_slots"]))
                        m = take(s)
                        for i, g in enumerate(groups_of(s)):
                            for t in range(T):
                                h = t * H + g * HB
                                ins = pe.transpose(bf(m)[:, i * S + t * 128:i * S + t * 128 + 128],
                                                   qs[L["W"]][j][:, h:h + HB, :], identb[:, :])
                        ins.then_inc(misc_filled[m], 1)
                    if s.kind == "A":
                        p3 = find(steps, "P3", s, 1 + s.q // 2)
                        for name in p3.misc:
                            drained(p3, name)
                        for n in range(units(s)[0]):
                            reuse("a_drained", s.a + n, A_BANKS)
                            ps = psA[:, (s.a + n) % A_BANKS, :]
                            if L["cross"]:
                                for t in range(T):
                                    for i in range(2):
                                        g = 2 * s.q + i
                                        lo = (2 * t + i) * 128
                                        ins = pe.matmul(ps[:, lo:lo + 128], QT[j][:, g, t * 128:t * 128 + 128],
                                                        kblk[s.L][j][:, g * L["KG"] // 8, :], start=True, stop=True)
                            else:
                                h = 4 * s.q + n
                                kg = (h // L["HB"]) % L["KG"]
                                for t in range(T):
                                    ins = pe.matmul(ps[:, t * S:t * S + S], qblk[s.L][j][:, h, t * 128:t * 128 + 128],
                                                    KT[j][:, kg, :], start=True, stop=True)
                            ins.then_inc(a_filled, 1)
                    if s.kind == "S":
                        half = 2 * s.q // (4 if L["cross"] else 8)
                        drained(find(steps, "N", s, 2 * half + 1))
                        for n in range(units(s)[1]):
                            reuse("b_drained", s.b + n, B_BANKS)
                            ps = psB[:, (s.b + n) % B_BANKS, :]
                            if L["cross"]:
                                for i in range(2):
                                    g = 2 * s.q + i
                                    ins = pe.matmul(ps[:, i * S:i * S + S], kblk[s.L][j][:, g * L["KG"] // 8, :], QT[j][:, g, :],
                                                    start=True, stop=True)
                            else:
                                h, kc = 4 * (s.q // 2) + 2 * n, s.q % 2
                                kg = (h // L["HB"]) % L["KG"]
                                ins = pe.matmul(ps, KT[j][:, kg, kc * 128:kc * 128 + 128],
                                                qblk[s.L][j][:, h:h + 2, :].rearrange("p a s -> p (a s)"), start=True, stop=True)
                            ins.then_inc(b_filled, 1)
                    if s.kind == "V":
                        sc = find(steps, "S", s, s.q)
                        nu = units(sc)[1]
                        pe.wait_ge(b_drained, value(pair, "b_drained", sc.b + nu))
                        if s.q == 0:
                            name = f"ot_drained{j}"
                            pe.wait_ge(ot_drained[j], value(pair, name, find(steps, "F1", s).after[name] - 1))
                        if L["cross"]:
                            for i in range(2):
                                g = 2 * s.q + i
                                c, u = g % 4, g // 4
                                ins = pe.matmul(psO[32 * c:32 * c + 32, j, u, :], vx[s.L][j][:, g, :], P[:, sc.p[0], i, :],
                                                start=True, stop=True, skip_group_check=True)
                        else:
                            four, kc = s.q // 2, s.q % 2
                            u, half = four // 2, four % 2
                            nh = 16 if s.L == "s0" else 8
                            for c in range(4):
                                lo = (kc * nh + (4 * four + c) % nh) * 32
                                ins = pe.matmul(psO[32 * c:32 * c + 32, j, u, :], vp[s.L][j][:, lo:lo + 32],
                                                P[:, sc.p[c // 2], c % 2, :],
                                                start=(half == 0 and kc == 0), stop=(half == 1 and kc == 1), skip_group_check=True)
                        ins.then_inc(p_used, nu)
                    if s.kind == "F1":
                        name = f"ot_drained{j}"
                        pe.wait_ge(ot_drained[j], value(pair, name, s.after[name]))
                        m = take(s)
                        for n in range(4):
                            t, u = n // 2, n % 2
                            ins = pe.transpose(psM[:, m, n * 128:n * 128 + 128], ots[j][:, u, t * 128:t * 128 + 128], wc_("ident"))
                        ins.then_inc(misc_filled[m], 1)
                    if s.kind == "F2":
                        drained(find(steps, "F1", s))
                        m = take(s)
                        to_columns(m, on4[j] if s.L == "s0" else on[j]).then_inc(misc_filled[m], 1)
                    if s.kind == "F3":
                        drained(find(steps, "F2", s))
                        m = take(s)
                        if s.L == "s0":
                            ins = pe.matmul(psM[:, m, 0:S], wc_("s0o"), onT[j][:, :], start=True, stop=True)
                        else:
                            for t in range(T):
                                ins = pe.matmul(psM[:, m, t * D:t * D + D], onT[j][:, t * 128:t * 128 + 128], wc_(s.L + "o"), start=True, stop=True)
                        ins.then_inc(misc_filled[m], 1)
                    if s.kind == "R1" and s.q == 0:
                        drained(find(steps, "F3", s))
                        m = take(s)
                        for t in range(T):
                            ins = pe.matmul(psM[:, m, t * E:t * E + E], mlaT[j][:, t * 128:t * 128 + 128], wc_("router"), start=True, stop=True)
                        ins.then_inc(misc_filled[m], 1)
                    if s.kind == "R2":
                        pe.wait_ge(gates_ready, value(pair, "gates_ready", s.after["gates_ready"]))
                        m = take(s)
                        to_columns(m, gate[j]).then_inc(misc_filled[m], 1)
                    if s.kind == "R3":
                        drained(find(steps, "R2", s))
                        m = take(s)
                        for t in range(T):
                            ins = pe.matmul(psM[:, m, t * D:t * D + D], gateT[j][:, t * 128:t * 128 + 128], b2[:, :], start=True, stop=True)
                        ins.then_inc(misc_filled[m], 1)
                    if s.kind == "G":
                        if s.L == "f" and s.q == 0:
                            drained(find(steps, "P1", s))
                        src, w = (mlaT[j], w1) if s.L == "s0" else (xnT[j], fw1)
                        reuse("b_drained", s.b, B_BANKS)
                        for f in range(2):
                            n = 2 * s.q + f
                            ins = pe.matmul(psB[:, s.b % B_BANKS, f * S:f * S + S], w[:, n * 128:n * 128 + 128], src[:, :], start=True, stop=True)
                        ins.then_inc(b_filled, 1)
                    if s.kind == "H":
                        gs = [find(steps, "G", s, s.q)] if s.L == "s0" else [find(steps, "G", s, 0), find(steps, "G", s, 1)]
                        w = w2 if s.L == "s0" else fw2
                        pe.wait_ge(b_drained, value(pair, "b_drained", gs[-1].b + 1))
                        reuse("a_drained", s.a, A_BANKS)
                        last = 2 * len(gs) - 1
                        for t in range(T):
                            for n in range(last + 1):
                                g = gs[n // 2]
                                k = 2 * s.q + n
                                ins = pe.matmul(psA[:, s.a % A_BANKS, t * D:t * D + D], P[:, g.p[0], n % 2, t * 128:t * 128 + 128],
                                                w[:, k * D:k * D + D], start=(n == 0), stop=(n == last))
                        ins.then_inc(a_filled, 1)


def kernel(**inputs):
    from concourse import bacc
    from concourse.bass_utils import run_bass_kernel_spmd

    g = {k: np.asarray(v) for k, v in inputs.items()}
    f32 = np.float32

    def pack(table, parts):
        assert [n for n, _ in table] == list(parts), [n for n, _ in table]
        out = [np.asarray(parts[n], f32).reshape(-1, w) for n, w in table]
        return np.ascontiguousarray(np.concatenate(out, axis=1))

    heads4 = lambda w: w.reshape(w.shape[0], H, 8)[:, :, :4].reshape(w.shape[0], 64)
    w = pack(W_COLS, {
        "ident": np.eye(128, dtype=f32), "ones": np.full((128, 128), 1.0 / D, f32),
        "bx": g["L0_attn_b_in"][:D], "bz": g["L0_attn_b_in"][D:], "dskip": g["L0_attn_D_skip"],
        "lng": g["L0_attn_ln_g"], "lnb": g["L0_attn_ln_b"], "rmsg": g["L1_attn_g"], "mlab": g["L0_ffn_o_b"],
        "logdt": g["L0_attn_log_dt"], "alog": g["L0_attn_A_log"],
        "b1": g["L0_ffn_b1"].reshape(16, 128).T, "fb1": g["L1_ffn_b1"].reshape(4, 128).T,
        "win": g["L0_attn_W_in"].T, "wb": g["L0_attn_W_B"].T, "wout": g["L0_attn_W_out"].T,
        "x0q": g["L0_xattn_w_q"].T, "x0k": g["L0_xattn_w_k"].T, "x0v": g["L0_xattn_w_v"].T, "x0o": g["L0_xattn_w_o"].T,
        "x1q": g["L1_xattn_Wq"].T, "x1k": g["L1_xattn_Wk"].T, "x1v": g["L1_xattn_Wv"].T, "x1o": g["L1_xattn_Wo"].T,
        "s0qk": np.concatenate([heads4(g["L0_ffn_q_w"]), g["L0_ffn_k_w"]], axis=1), "s0v": g["L0_ffn_v_w"], "s0o": g["L0_ffn_o_w"],
        "router": g["L0_ffn_router_w"],
        "s1qk": np.concatenate([g["L1_attn_w_q"], g["L1_attn_w_k"]], axis=1), "s1v": g["L1_attn_w_v"], "s1o": g["L1_attn_w_o"],
    })
    twice = lambda v: np.concatenate([v, v])
    rows = pack(R_COLS, {
        "iota": np.arange(S, dtype=f32),
        "bout": g["L0_attn_b_out"], "x0bq": twice(g["L0_xattn_b_q"]), "x0bk": g["L0_xattn_b_k"], "x0bv": g["L0_xattn_b_v"],
        "x0bo": g["L0_xattn_b_o"], "x1bq": twice(g["L1_xattn_bq"]), "x1bk": g["L1_xattn_bk"], "x1bv": g["L1_xattn_bv"],
        "x1bo": g["L1_xattn_bo"], "s0bq": twice(heads4(g["L0_ffn_q_b"][None])[0]), "s0bk": twice(g["L0_ffn_k_b"]),
        "s0bv": twice(g["L0_ffn_v_b"]), "rb": twice(g["L0_ffn_router_b"]), "fb2": g["L1_ffn_b2"],
        "tri": twice(np.tril(np.ones((E, E), f32), -1).reshape(-1)),
    })[0]
    pos, dims = np.arange(S, dtype=f32), np.arange(8)
    theta = np.power(f32(10000.0), (-2.0 * (dims // 2) / 8).astype(f32)).astype(f32)
    ang = (pos[:, None] * theta[None, :]).astype(f32)
    sign = np.where(np.arange(S) % 2 == 1, -1.0, 1.0).astype(f32)
    rf = np.cos(ang) + sign[:, None] * np.sin(ang)
    freq = (1.0 / f32(10000.0) ** (np.arange(0, 8, 2, dtype=f32) / f32(8))).astype(f32)
    emb = np.concatenate([np.outer(pos, freq)] * 2, axis=1).astype(f32)
    cos = np.cos(emb)
    sin = np.sin(emb) * np.where(dims < 4, -1.0, 1.0).astype(f32)
    tiles = lambda t: t.reshape(T, 128, 8).transpose(1, 0, 2).reshape(128, 16)
    rope = pack(T_COLS, {"rf": tiles(rf), "qcos": tiles(cos), "qsin": tiles(sin),
                         "kcos": np.concatenate([cos[:C]] * 2), "ksin": np.concatenate([sin[:C]] * 2)})
    wc = np.zeros((128, D), f32)
    for c in range(4):
        wc[32 * c:32 * c + NS] = g["L0_attn_W_C"].T
    b2 = np.zeros((128, D), f32)
    b2[:E] = g["L0_ffn_b2"]
    arrays = {
        "x": g["x"],
        "context": g["ctx_1024"].reshape(PAIRS, 2, C, D).transpose(3, 0, 1, 2),
        "weights": w,
        "expert_w1": g["L0_ffn_w1"].transpose(1, 0, 2).reshape(D, -1),
        "expert_w2": g["L0_ffn_w2"].reshape(E, 2, 128, D).transpose(2, 0, 1, 3).reshape(128, -1),
        "expert_b2": b2,
        "mlp_w1": g["L1_ffn_w1"],
        "mlp_w2": g["L1_ffn_w2"].reshape(4, 128, D).transpose(1, 0, 2).reshape(128, -1),
        "state_out": wc,
        "bias_rows": rows,
        "positions": rope,
        "flip": np.eye(128, dtype=f32)[::-1],
    }
    arrays = {k: np.ascontiguousarray(v) for k, v in arrays.items()}
    nc = bacc.Bacc("TRN2", target_bir_lowering=False, num_devices=1)
    aps = [nc.dram_tensor(n, a.shape, mybir.dt.from_np(a.dtype), kind="ExternalInput").ap() for n, a in arrays.items()]
    out = nc.dram_tensor("y", (B, S, D), F32, kind="ExternalOutput").ap()
    decoder(nc, *aps, out)
    result = run_bass_kernel_spmd(nc, [arrays], core_ids=[0])
    return result.results[0]["y"]
```
